# Optimizing a Trainium2 kernel written in Bass

```python
import numpy as np
import jax
import jax.numpy as jnp

def _softmax(x, axis=-1):
    return jax.nn.softmax(x, axis=axis)

def _gelu(x):
    return jax.nn.gelu(x, approximate=True)

def _silu(x):
    return jax.nn.silu(x)

def _sigmoid(x):
    return jax.nn.sigmoid(x)

def _layernorm(x, axis=-1, eps=1e-05):
    m = jnp.mean(x, axis=axis, keepdims=True)
    v = jnp.var(x, axis=axis, keepdims=True)
    return (x - m) / jnp.sqrt(v + eps)

def _scatter_add(tgt, idx, src, axis=0):
    return tgt.at[idx].add(src)

def _segment_sum(src, seg, n):
    return jax.ops.segment_sum(src, seg, n)
kernel_name = 'mk_gnn_resnorm_d2_gnn_r32_5ad928'

def setup_inputs(seed: int=0):
    np.random.seed(seed)
    _w = jnp.asarray

    def _rec_inputs():
        import jax
        import jax.numpy as jnp
        _gk = jax.random.key(seed)
        x = -0.0002117 + 1 * jax.random.normal(jax.random.fold_in(_gk, 1), (3125, 256), jnp.float32)
        src = jax.random.randint(jax.random.fold_in(_gk, 2), (50000,), 0, 3125, jnp.int32)
        dst = jnp.minimum((3125 * jax.random.uniform(jax.random.fold_in(_gk, 3), (50000,)) ** 2.0).astype(jnp.int32), 99999)
        _o = jnp.argsort(dst, stable=True)
        src = src[_o]
        dst = dst[_o]
        return (x, src, dst)
    x, src, dst = _rec_inputs()

    def _L0_gnn_setup():
        import jax, jax.numpy as jnp
        import numpy as np
        N_NODES = 3125
        N_EDGES = 50000
        D = 256

        def _gcn_conv(x, src, dst, W, b, n):
            xw = x @ W
            ones = jnp.ones(dst.shape, dtype=xw.dtype)
            deg = jax.ops.segment_sum(ones, dst, num_segments=n) + 1.0
            dinv = jax.lax.rsqrt(deg)
            coef = dinv[src] * dinv[dst]
            msg = xw[src] * coef[:, None]
            agg = jax.ops.segment_sum(msg, dst, num_segments=n)
            self_loop = (dinv * dinv)[:, None] * xw
            return agg + self_loop + b
        key = jax.random.key(seed)
        ks = jax.random.split(key, 8)
        scale = 1.0 / np.sqrt(D)
        x = jax.random.normal(ks[0], (N_NODES, D), dtype=jnp.float32)
        edge_index = jax.random.randint(ks[1], (2, N_EDGES), 0, N_NODES, dtype=jnp.int64)
        W1 = jax.random.normal(ks[2], (D, D), dtype=jnp.float32) * scale
        b1 = jnp.zeros((D,), dtype=jnp.float32)
        W2 = jax.random.normal(ks[3], (D, D), dtype=jnp.float32) * scale
        b2 = jnp.zeros((D,), dtype=jnp.float32)
        W3 = jax.random.normal(ks[4], (D, D), dtype=jnp.float32) * scale
        b3 = jnp.zeros((D,), dtype=jnp.float32)
        return {'x': x, 'edge_index': edge_index, 'W1': W1, 'b1': b1, 'W2': W2, 'b2': b2, 'W3': W3, 'b3': b3}
    _L0_gnn_all = _L0_gnn_setup()
    _L0_gnn_in = {k: v for k, v in _L0_gnn_all.items() if k in ('W1', 'b1', 'W2', 'b2', 'W3', 'b3')}
    del _L0_gnn_all

    def _L1_gnn_setup():
        import jax, jax.numpy as jnp
        import numpy as np
        N = 3125
        E = 50000
        IN_FEATS = 256
        OUT_FEATS = 256
        MAXK = 32

        def _maxk(x, k):
            _, idx = jax.lax.top_k(x, k)
            rows = jnp.arange(x.shape[0])[:, None]
            mask = jnp.zeros_like(x).at[rows, idx].set(1.0)
            return x * mask
        key = jax.random.key(seed)
        k1, k2, k3, k4, k5 = jax.random.split(key, 5)
        feat = jax.random.normal(k1, (N, IN_FEATS), dtype=jnp.float32)
        W_self = jax.random.normal(k2, (IN_FEATS, OUT_FEATS), dtype=jnp.float32) * (1.0 / np.sqrt(IN_FEATS))
        W_neigh = jax.random.normal(k3, (IN_FEATS, OUT_FEATS), dtype=jnp.float32) * (1.0 / np.sqrt(IN_FEATS))
        src = jax.random.randint(k4, (E,), 0, N, dtype=jnp.int64)
        dst = jax.random.randint(k5, (E,), 0, N, dtype=jnp.int64)
        return {'feat': feat, 'W_self': W_self, 'W_neigh': W_neigh, 'src': src, 'dst': dst}
    _L1_gnn_all = _L1_gnn_setup()
    _L1_gnn_in = {k: v for k, v in _L1_gnn_all.items() if k in ('W_self', 'W_neigh')}
    del _L1_gnn_all
    return {'x': x, 'src': src, 'dst': dst, 'L0_gnn_W1': _L0_gnn_in['W1'], 'L0_gnn_b1': _L0_gnn_in['b1'], 'L0_gnn_W2': _L0_gnn_in['W2'], 'L0_gnn_b2': _L0_gnn_in['b2'], 'L0_gnn_W3': _L0_gnn_in['W3'], 'L0_gnn_b3': _L0_gnn_in['b3'], 'L1_gnn_W_self': _L1_gnn_in['W_self'], 'L1_gnn_W_neigh': _L1_gnn_in['W_neigh']}

def reference(x, src, dst, L0_gnn_W1, L0_gnn_b1, L0_gnn_W2, L0_gnn_b2, L0_gnn_W3, L0_gnn_b3, L1_gnn_W_self, L1_gnn_W_neigh):
    import jax
    import jax.numpy as jnp

    def _L0_gnn_ref(x, edge_index, W1, b1, W2, b2, W3, b3):
        import jax, jax.numpy as jnp
        import numpy as np
        N_NODES = 3125
        N_EDGES = 50000
        D = 256

        def _gcn_conv(x, src, dst, W, b, n):
            xw = x @ W
            ones = jnp.ones(dst.shape, dtype=xw.dtype)
            deg = jax.ops.segment_sum(ones, dst, num_segments=n) + 1.0
            dinv = jax.lax.rsqrt(deg)
            coef = dinv[src] * dinv[dst]
            msg = xw[src] * coef[:, None]
            agg = jax.ops.segment_sum(msg, dst, num_segments=n)
            self_loop = (dinv * dinv)[:, None] * xw
            return agg + self_loop + b
        src, dst = (edge_index[0], edge_index[1])
        n = x.shape[0]
        h = jax.nn.relu(_gcn_conv(x, src, dst, W1, b1, n))
        h = jax.nn.relu(_gcn_conv(h, src, dst, W2, b2, n))
        return _gcn_conv(h, src, dst, W3, b3, n)

    def _L1_gnn_ref(feat, W_self, W_neigh, src, dst):
        import jax, jax.numpy as jnp
        import numpy as np
        N = 3125
        E = 50000
        IN_FEATS = 256
        OUT_FEATS = 256
        MAXK = 32

        def _maxk(x, k):
            _, idx = jax.lax.top_k(x, k)
            rows = jnp.arange(x.shape[0])[:, None]
            mask = jnp.zeros_like(x).at[rows, idx].set(1.0)
            return x * mask
        n = feat.shape[0]
        h_self = feat @ W_self
        h_neigh = feat @ W_neigh
        h_sparse = _maxk(h_neigh, MAXK)
        msg = h_sparse[src]
        summed = jax.ops.segment_sum(msg, dst, num_segments=n)
        deg = jax.ops.segment_sum(jnp.ones((src.shape[0],), dtype=feat.dtype), dst, num_segments=n)
        neigh = summed / jnp.maximum(deg, 1.0)[:, None]
        return h_self + neigh
    edge_index = jnp.stack([src, dst])
    x = _layernorm(x + _L0_gnn_ref(x, edge_index, L0_gnn_W1, L0_gnn_b1, L0_gnn_W2, L0_gnn_b2, L0_gnn_W3, L0_gnn_b3), axis=-1)
    x = _layernorm(x + _L1_gnn_ref(x, L1_gnn_W_self, L1_gnn_W_neigh, src, dst), axis=-1)
    return x

_drawn_inputs = setup_inputs


def setup_inputs(seed=0):
    import zlib

    import numpy as np

    out = dict(_drawn_inputs(seed))
    spreads = {'L0_gnn_b1': (0.0, 0.1), 'L0_gnn_b2': (0.0, 0.1), 'L0_gnn_b3': (0.0, 0.1)}
    factors = {'L0_gnn_W1': 2.835}
    for name, (base, spread) in spreads.items():
        noise = np.random.default_rng([zlib.crc32(name.encode()), seed]).standard_normal(out[name].shape)
        drawn = base * np.exp(spread * noise) if base else spread * noise
        out[name] = jnp.asarray(drawn.astype(out[name].dtype))
    for name, factor in factors.items():
        out[name] = (out[name] * factor).astype(out[name].dtype)
    return out
```

```python
import numpy as np
import concourse.bass as bass
from concourse import mybir
from concourse.alu_op_type import AluOpType as ALU

F32 = mybir.dt.float32
F16 = mybir.dt.float16
I32 = mybir.dt.int32
ACT = mybir.ActivationFunctionType

N = 3125
E = 50000
D = 256
TR = 125
NT = N // TR
HB = D // 128

WIN = 20
NW = -(-N // WIN)
AC = NW * WIN
GE = 256
NG = -(-E // GE)
GK = -(-NG // 128)
GL = NG - 128 * (GK - 1)
ELAST = E - GE * (NG - 1)
NS = NW + NG - 1
AHEAD = 3
RING = AHEAD + 1
NSP = NS + RING
UNROLL = 8
assert NS % UNROLL == 0 and E % 128 < 256 and GK == 2
NOWHERE = 40000
ROUND = 1.5 * 2 ** 23

CT = 4
CW = CT * TR
NC = 1 + (NT - 1) // CT
TOPK = 32
GONE = -3.0e38


def chunk(i):
    if isinstance(i, int) and i < 2:
        return (1, CT) if i == 0 else (0, 1)
    return CT * i - (CT - 1), CT


def first_of(i):
    if isinstance(i, int) and i < 2:
        return CT * i
    return CT * i - (CT - 1)


def gnn(nc, x, src, dst, w1, b1, w2, b2, w3, b3, wself, wneigh, out):
    def sb(name, shape, dt):
        return nc.alloc_sbuf_tensor(name, shape, dt).ap()

    def sem(name):
        return nc.alloc_semaphore(name)

    xparts_dram = [nc.dram_tensor(f"xparts{l}", (NT, TR, 2 * D), F16, kind="Internal").ap() for l in range(3)]
    base_dram = nc.dram_tensor("base", (NT, TR, D), F32, kind="Internal").ap()

    AT = sb("AT", [128, NT * AC], F16)
    X = sb("X", [128, NT * 2 * D], F16)
    S = sb("S", [128, 14 * D], F32)
    W = sb("W", [128, HB, 2 * D], F32)
    W3 = sb("W3", [128, HB, D], F32)
    DG = sb("DG", [128, CT * TR], F32)
    B12 = sb("B12", [128, 2, D], F32)
    B3 = sb("B3", [128, D], F32)
    ident = sb("ident", [128, 128], F32)
    ident16 = sb("ident16", [128, TR], F16)
    zero16 = sb("zero16", [128, TR], F16)
    one16 = sb("one16", [128, 1], F16)
    one32 = sb("one32", [128, 1], F32)
    tabs = sb("tabs", [128, 8, NT], F32)
    deg, dinv, sdeg, rdeg, rneigh = (tabs[0:TR, i, :] for i in range(5))
    mhalf = tabs[0:TR, 5, :]
    phalf = tabs[0:TR, 6, :]
    steps_off = sb("steps_off", [1, NS], I32)
    stats = sb("stats", [128, CT, 6], F32)
    mv = sb("mv", [128, CT, 2], F32)
    rstd = sb("rstd", [128, CT], F32)
    top8 = sb("top8", [128, TOPK // 8, 8], F32)

    ATt = AT.rearrange("p (t c) -> p t c", t=NT)
    Xt = X.rearrange("p (t a d) -> p t a d", t=NT, a=2)
    St = S.rearrange("p (k d) -> p k d", d=D)
    DGt = DG.rearrange("p (j n) -> p j n", j=CT)

    keyhot = X[:, 0:RING * 2 * 500].rearrange("p (r h n) -> p r h n", r=RING, h=2)
    o = RING * 2 * 500
    lohot = X[:, o:o + RING * 2 * 126].rearrange("p (r h n) -> p r h n", r=RING, h=2)
    o += RING * 2 * 126
    counted = X[:, o:o + RING * 500].rearrange("p (r n) -> p r n", r=RING)
    o += RING * 500
    ints = X[:, o:o + 4 * 2 * GE].bitcast(I32).rearrange("p (q k e) -> p q k e", q=2, k=2)
    o += 4 * 2 * GE
    flts = X[:, o:o + 4 * 2 * GE].bitcast(F32).rearrange("p (q k e) -> p q k e", q=2, k=2)
    o += 4 * 2 * GE
    grouphot = X[:, o:o + 2 * NS].rearrange("p (k s) -> p k s", k=2)
    o += 2 * NS
    assert o <= NT * 2 * D
    KEYS = NT * WIN
    hi = X[:, 0:1024].bitcast(F32).rearrange("p (k e) -> p k e", k=2)
    wd = X[:, 1024:2048].bitcast(F32).rearrange("p (k e) -> p k e", k=2)
    q16 = X[:, 2048:2048 + 3 * 2 * GE].rearrange("p (q k e) -> p q k e", q=3, k=2)
    gcol16 = X[:, 3584:3584 + 256].rearrange("p (k m) -> p k m", k=2)
    assert 3840 <= RING * 2 * 500

    o = 0
    steptab = S[:, o:o + 4 * NSP].rearrange("p (q h s) -> p q h s", q=2, h=2)
    o += 4 * NSP
    iota_s = S[:, o:o + NS]
    o += NS
    bstep = S[:, o:o + NS]
    o += NS
    iota_key = S[:, o:o + KEYS // 2].bitcast(F16)
    o += KEYS // 2
    iota_lo = S[:, o:o + 64].bitcast(F16)
    o += 64
    lastd = S[:, o:o + 4].bitcast(I32)
    o += 4
    gend = S[:, o:o + 2]
    o += 2
    gprev = S[:, o:o + 2]
    o += 2
    gidx = S[:, o:o + 2]
    o += 2
    turn_lo = S[:, o:o + 2 * UNROLL].rearrange("p (h u) -> p h u", h=2)
    o += 2 * UNROLL
    tmpk = S[:, o:o + NS]
    o += NS
    assert o <= 14 * D, o

    P = nc.alloc_psum_tensor("P", [128, 8, 512], F32).ap()

    s_edges = sem("edges_loaded")
    s_prev = sem("previous_dst_loaded")
    s_wts = sem("weights_loaded")
    s_pc = sem("pool_constants_ready")
    s_dc = sem("dve_constants_ready")
    s_v = sem("dve_step_done")
    s_p = sem("pool_step_done")
    s_zero = sem("at_zeroed")
    s_sel = sem("edges_selected")
    s_tab = sem("step_tables_ready")
    s_key = sem("keyhot_ready")
    s_lo = sem("lohot_ready")
    s_turn = sem("turn_columns_copied")
    s_cnt = sem("window_counted")
    s_cp = sem("counted_copied")
    s_add = sem("counted_added")
    s_diag = sem("self_loops_added")
    s_drow = sem("degree_row_summed")
    s_dcp = sem("degree_row_copied")
    s_dcol = sem("degree_columns_ready")
    s_degc = sem("degrees_copied")
    s_pow = sem("degree_powers_ready")
    s_rd = sem("degree_tables_ready")
    s_xl = [sem(f"x_loaded{i}") for i in range(2)]
    s_xh = sem("x1_high_ready")
    s_x1 = sem("x1_parts_ready")
    s_aev = sem("chunk_evacuated")
    s_dg = sem("diagonals_ready")
    s_w1 = sem("w1_applied")
    s_h = sem("hidden_ready")
    s_wx = sem("next_operand_multiplied")
    s_ph = sem("high_parts_ready")
    s_pl = sem("low_parts_ready")
    s_st = sem("parts_stored")
    s_st3 = [sem(f"last_parts_stored{i}") for i in range(2)]
    s_used = sem("operand_tiles_used")
    s_re = [sem(f"operand_reloaded{i}") for i in range(NC)]
    s_xr = [sem(f"residual_loaded{i}") for i in range(2)]
    s_xb = sem("residual_and_bias_ready")
    s_mv = sem("mean_and_variance_ready")
    s_rs = sem("rstd_ready")
    s_ln = sem("normalised")
    s_tr = sem("x1_transposed")
    s_tc = sem("x1_transpose_copied")
    s_hh = sem("self_and_neighbour_ready")
    s_hn = sem("neighbour_copied")
    s_bs = sem("base_ready")
    s_bst = [sem(f"base_stored{i}") for i in range(2)]
    s_sp = sem("sparse_ready")
    s_wn = sem("neighbour_weights_loaded")
    s_nd = sem("self_loops_removed")
    s_topk = sem("topk_step_done")
    s_out = [sem(f"out_stored{i}") for i in range(2)]

    def edge_rows(a, k):
        n = 128 if k == 0 else GL - 1
        return a[128 * k * GE:(128 * k + n) * GE].rearrange("(g e) -> g e", e=GE), n

    def parts_rows(l, t0, nt):
        return xparts_dram[l][bass.ds(t0, nt), :, :].rearrange("t p e -> p t e")

    def tile_rows(a, t0, nt):
        return a[bass.ds(t0, nt), :, :].rearrange("t p d -> p t d")

    x_t = x.rearrange("(t p) d -> t p d", p=TR)
    out_t = out.rearrange("(t p) d -> t p d", p=TR)
    parts_out = S[:, 8 * D:12 * D].bitcast(F16).rearrange("p (j a d) -> p j a d", j=CT, a=2)
    aggT = St[:, 0:4, :].rearrange("p k d -> p (k d)")[:, 0:2 * CW].rearrange("p (h n) -> p h n", h=2)
    hT = St[:, 4:8, :].rearrange("p k d -> p (k d)")[:, 0:2 * CW].rearrange("p (h n) -> p h n", h=2)
    NXG = -(-NT // 4)

    def chunks(eng, step):
        for i in range(3):
            step(i, i)
        with eng.Fori(0, (NC - 3) // 2) as turn:
            step(2 * turn + 3, 3)
            step(2 * turn + 4, 4)

    def slot2(k, j):
        return (first_of(k) + j) % 2

    def ring_slots(k, nt):
        return St[0:TR, 4 * (k % 2):4 * (k % 2) + nt, :]

    def ring_tile(k, j):
        return St[0:TR, 4 * (k % 2) + j, :]

    last_parts = [St[0:TR, 8 + r, :].bitcast(F16).rearrange("p (a d) -> p a d", a=2) for r in range(2)]
    neigh_row = St[0:TR, 10, :]
    neigh_left = St[0:TR, 11, :]
    sparse_row = St[0:TR, 12, :]
    x1T = [DG[:, r * 2 * TR:(r + 1) * 2 * TR].rearrange("p (h n) -> p h n", h=2) for r in range(2)]

    def agg_bank(li, h):
        return P[:, 2 * (li % 2) + h, :]

    with nc.Block() as block:

        @block.sync
        def _(sp):
            for q, a in ((0, src), (1, dst)):
                rows, n = edge_rows(a, 0)
                sp.dma_start(ints[0:n, q, 0, :], rows).then_inc(s_edges, 16)
            sp.wait_ge(s_dc, 1)
            for q, a in ((0, src), (1, dst)):
                rows, n = edge_rows(a, 1)
                sp.dma_start(ints[0:n, q, 1, :], rows).then_inc(s_edges, 16)
                sp.dma_start(ints[n:n + 1, q, 1, 0:ELAST],
                             a[GE * (NG - 1):E].rearrange("(g e) -> g e", g=1)).then_inc(s_edges, 16)
            last = dst[0:(NG - 1) * GE].rearrange("(g e) -> g e", e=GE)[:, GE - 1:GE]
            sp.dma_start(lastd[1:128, 0:1], last[0:127, :],
                         allow_slow_non_contiguous=True).then_inc(s_prev, 16)
            sp.dma_start(lastd[0:GL, 1:2], last[127:NG - 1, :],
                         allow_slow_non_contiguous=True).then_inc(s_prev, 16)
            for a, dest in ((w1, W[:, :, 0:D]), (w2, W[:, :, D:2 * D]), (w3, W3[:, :, :])):
                sp.dma_start(dest, a.rearrange("(h p) d -> p h d", p=128)).then_inc(s_wts, 16)
            for a, dest in ((b1, B12[:, 0, :]), (b2, B12[:, 1, :]), (b3, B3[:, :])):
                sp.dma_start(dest, a.rearrange("(o d) -> o d", o=1).broadcast_to([128, D])).then_inc(s_wts, 16)
            sp.wait_ge(s_add, NS + 1)
            for g in range(NXG):
                nt = min(4, NT - 4 * g)
                if g >= 2:
                    sp.wait_ge(s_x1, 4 * (g - 1))
                sp.dma_start(St[0:TR, 4 * (g % 2):4 * (g % 2) + nt, :],
                             tile_rows(x_t, 4 * g, nt)).then_inc(s_xl[g % 2], 16)

            def reload(l):
                for q in range(NC):
                    t0, nt = (0, 1) if q == 0 else (4 * q - 3, CT)
                    i = {0: 1, 1: 0}.get(q, q)
                    if l < 2:
                        sp.wait_ge(s_st, 16 * (NC * l + max(i + 1, 2 if q < 2 else 0)))
                    else:
                        done = first_of(i) + nt
                        sp.wait_ge(s_st3[0], 16 * ((done + 1) // 2))
                        sp.wait_ge(s_st3[1], 16 * (done // 2))
                    sp.wait_ge(s_used, NC * NC * l + NC * (NC - 1) + q + 1)
                    sp.dma_start(Xt[0:TR, t0:t0 + nt, :, :].rearrange("p t a d -> p t (a d)"),
                                 parts_rows(l, t0, nt)).then_inc(s_re[q], 16)

            for l in range(2):
                for i in range(NC):
                    t0, nt = chunk(i)
                    sp.wait_ge(s_ph, NT * l + first_of(i) + nt)
                    sp.wait_ge(s_pl, NT * l + first_of(i) + nt)
                    sp.dma_start(parts_rows(l, t0, nt),
                                 parts_out[0:TR, 0:nt, :, :].rearrange("p j a d -> p j (a d)")).then_inc(s_st, 16)
                    if l == 0 and i == NC - 1:
                        sp.wait_ge(s_wx, NC)
                        for a, dest in ((wself, W[:, :, 0:D]), (wneigh, W[:, :, D:2 * D])):
                            sp.dma_start(dest, a.rearrange("(h p) d -> p h d", p=128)).then_inc(s_wn, 16)
                reload(l)

            def load_ring(i, rows):
                t0, nt = chunk(i)
                sp.dma_start(ring_slots(i, nt), tile_rows(rows, t0, nt)).then_inc(s_xr[i % 2], 16)

            sp.wait_ge(s_wx, 2 * NC)
            load_ring(0, x_t)
            load_ring(1, x_t)
            for i in range(NC):
                t0, nt = chunk(i)
                for j in range(nt):
                    o = first_of(i) + j
                    sp.wait_ge(s_bs, o + 1)
                    sp.dma_start(tile_rows(base_dram, t0 + j, 1), ring_slots(i, nt)[:, j:j + 1, :]
                                 ).then_inc(s_bst[i % 2], 16)
                    sp.wait_ge(s_ph, 2 * NT + o + 1)
                    sp.wait_ge(s_pl, 2 * NT + o + 1)
                    sp.dma_start(parts_rows(2, t0 + j, 1), last_parts[o % 2].rearrange("p a d -> p (a d)")
                                 .unsqueeze(1)).then_inc(s_st3[o % 2], 16)
                if i + 2 < NC:
                    sp.wait_ge(s_bst[i % 2], 16 * sum(chunk(c)[1] for c in range(i % 2, i + 1, 2)))
                    load_ring(i + 2, x_t)
            reload(2)

            for r in range(2):
                sp.wait_ge(s_bst[r], 16 * sum(chunk(c)[1] for c in range(r, NC, 2)))
            load_ring(0, base_dram)
            load_ring(1, base_dram)
            for i in range(NC):
                t0, nt = chunk(i)
                sp.wait_ge(s_ln, NT + first_of(i) + nt)
                sp.dma_start(tile_rows(out_t, t0, nt), ring_slots(i, nt)).then_inc(s_out[i % 2], 16)
                if i + 2 < NC:
                    sp.wait_ge(s_out[i % 2], 16 * (i // 2 + 1))
                    load_ring(i + 2, base_dram)
            for r in range(2):
                sp.wait_ge(s_out[r], 16 * len(range(r, NC, 2)))

        @block.gpsimd
        def _(pool):
            done = [0]

            def link(ins):
                done[0] += 1
                ins.then_inc(s_p, 1)
                pool.wait_ge(s_p, done[0])

            link(pool.memset(ident[:, :], 0.0))
            link(pool.affine_select(out=ident[:, :], in_=ident[:, :], compare_op=ALU.not_equal, fill=1.0,
                                    base=0, pattern=[[-1, 128]], channel_multiplier=1))
            link(pool.iota(iota_s, pattern=[[1, NS]], base=0, channel_multiplier=0,
                           allow_small_or_imprecise_dtypes=True))
            link(pool.iota(gidx, pattern=[[128, 2]], base=0, channel_multiplier=1,
                           allow_small_or_imprecise_dtypes=True))
            link(pool.iota(iota_key, pattern=[[1, KEYS]], base=1, channel_multiplier=0,
                           allow_small_or_imprecise_dtypes=True))
            pool.iota(iota_lo, pattern=[[1, 128]], base=0, channel_multiplier=0,
                      allow_small_or_imprecise_dtypes=True).then_inc(s_pc, 1)
            half = NT * AC // 4
            pool.memset(AT[:, 0:2 * half].bitcast(F32), 0.0).then_inc(s_zero, 1)

            pool.wait_ge(s_tab, 1)
            pool.sem_inc(s_lo, 1)
            with pool.Fori(0, NS // UNROLL) as turn:
                s = turn * UNROLL
                pool.wait_ge(s_lo, s + 1)
                pool.nop(nofuse=True)
                pool.tensor_copy(turn_lo, steptab[:, 1, :, bass.ds(s, UNROLL)]).then_inc(s_turn, 1)
                pool.wait_ge(s_turn, turn + 1)
                for u in range(UNROLL):
                    pool.wait_ge(s_key, s + u + 1)
                    pool.nop(nofuse=True)
                    for h in range(2):
                        last = pool.tensor_scalar(lohot[:, u % RING, h, 0:TR], iota_lo[:, 0:TR],
                                                  turn_lo[:, h, u:u + 1], None, ALU.is_equal)
                    last.then_inc(s_lo, 1)

            pool.wait_ge(s_degc, 1)
            link(pool.tensor_tensor(dinv, deg, mhalf, ALU.pow))
            pool.tensor_tensor(sdeg, deg, phalf, ALU.pow).then_inc(s_pow, 1)

            def finish_rstd(k, li, nt):
                pool.wait_ge(s_mv, li + 1)
                pool.nop(nofuse=True)
                pool.tensor_scalar(rstd[0:TR, 0:nt], mv[0:TR, 0:nt, 1], 1e-5, None, ALU.add).then_inc(s_p, 1)
                pool.wait_ge(s_p, done[0] + 1 + li)
                pool.tensor_tensor(rstd[0:TR, 0:nt], rstd[0:TR, 0:nt], mhalf[:, 0:nt], ALU.pow).then_inc(s_rs, 1)

            def layer3(i, k):
                t0, nt = chunk(i)
                if k == 0:
                    pool.wait_ge(s_wts, 16 * 6)
                pool.wait_ge(s_xr[k % 2], 8 * (i + 2 - k % 2))
                pool.tensor_tensor(ring_slots(k, nt), ring_slots(k, nt),
                                   B3[0:TR, :].unsqueeze(1).broadcast_to([TR, nt, D]), ALU.add).then_inc(s_xb, 1)
                finish_rstd(k, i, nt)
                for j in range(nt):
                    o = first_of(i) + j
                    pool.wait_ge(s_ph, 2 * NT + o + 1)
                    pool.tensor_tensor(last_parts[slot2(k, j)][:, 1, :], sparse_row,
                                       last_parts[slot2(k, j)][:, 0, :], ALU.subtract).then_inc(s_pl, 1)

            chunks(pool, layer3)

            def layer4(i, k):
                finish_rstd(k, NC + i, chunk(i)[1])

            chunks(pool, layer4)

        @block.scalar
        def _(act):
            with act.Fori(0, NS // UNROLL) as turn:
                s = turn * UNROLL
                for u in range(UNROLL):
                    act.wait_ge(s_cnt, s + u + 1)
                    act.activation(counted[0:TR, u % RING, :], P[0:TR, u % RING, 0:KEYS], ACT.Copy).then_inc(s_cp, 1)

            for c in range(NXG):
                n = min(CW, N - CW * c)
                act.wait_ge(s_drow, c + 1)
                act.activation(S[0:1, 8 * D + 512 * (c % 2):8 * D + 512 * (c % 2) + n], P[0:1, c % 2, 0:n],
                               ACT.Copy).then_inc(s_dcp, 1)

            act.wait_ge(s_rd, 1)
            for t in range(NT):
                act.wait_ge(s_xl[t // 4 % 2], 16 * (t // 8 + 1))
                act.activation(Xt[0:TR, t, 0, :], St[0:TR, t % 8, :], ACT.Copy,
                               scale=dinv[:, t:t + 1]).then_inc(s_xh, 1)

            def high_parts(i, k, l):
                t0, nt = chunk(i)
                act.wait_ge(s_wx, NC * l + i + 1)
                if l or k:
                    act.wait_ge(s_st, 16 * (NC * l + i))
                for j in range(nt):
                    act.activation(parts_out[0:TR, j, 0, :], P[0:TR, 6 + j // 2, (j % 2) * D:(j % 2 + 1) * D],
                                   ACT.Copy, scale=rdeg[:, bass.ds(t0 + j, 1)]).then_inc(s_ph, 1)

            def layer1(i, k):
                t0, nt = chunk(i)
                act.wait_ge(s_used, NC * (i + 1))
                if k:
                    act.wait_ge(s_w1, i)
                act.activation(aggT[:, :, 0:nt * TR], P[:, 2 * (k % 2):2 * (k % 2) + 2, 0:nt * TR],
                               ACT.Copy).then_inc(s_aev, 1)
                high_parts(i, k, 0)

            chunks(act, layer1)
            chunks(act, lambda i, k: high_parts(i, k, 1))

            def layer3(i, k):
                nt = chunk(i)[1]

                def copy_transposed(j):
                    o = first_of(i) + j
                    act.wait_ge(s_tr, o + 1)
                    act.activation(x1T[slot2(k, j)], P[:, 4 + slot2(k, j), 0:2 * TR]
                                   .rearrange("p (h n) -> p h n", h=2), ACT.Copy).then_inc(s_tc, 1)

                copy_transposed(0)
                for j in range(nt):
                    o = first_of(i) + j
                    act.wait_ge(s_bs, o + 1)
                    if k or j:
                        act.wait_ge(s_sp, o)
                    act.activation(neigh_row, P[0:TR, 6 + slot2(k, j), D:2 * D], ACT.Copy).then_inc(s_hn, 1)
                    if j + 1 < nt:
                        copy_transposed(j + 1)
                    act.wait_ge(s_sp, o + 1)
                    if k >= 3:
                        act.wait_ge(s_st3[slot2(k, j)], 8 * (o - slot2(k, j)))
                    elif o >= 2:
                        act.wait_ge(s_st3[o % 2], 16 * (o // 2))
                    act.activation(last_parts[slot2(k, j)][:, 0, :], sparse_row, ACT.Copy).then_inc(s_ph, 1)

            chunks(act, layer3)

        @block.vector
        def _(dve):
            done = [0]

            def link(ins):
                done[0] += 1
                ins.then_inc(s_v, 1)
                dve.wait_ge(s_v, done[0])

            dve.memset(ints[0:GL, 0, 1, :], 0)
            link(dve.memset(ints[0:GL, 1, 1, :], NOWHERE))
            dve.memset(lastd[0:1, 0:1], 0)
            dve.memset(mhalf, -0.5)
            dve.memset(phalf, 0.5)
            dve.memset(zero16[:, :], 0.0)
            dve.memset(one16[:, :], 1.0)
            dve.memset(one32[:, :], 1.0).then_inc(s_dc, 1)
            quarter = NT * AC // 4
            dve.memset(steptab[:, :, :, NS:NSP], 0.0)
            dve.memset(AT[:, 2 * quarter:4 * quarter].bitcast(F32), 0.0).then_inc(s_zero, 1)

            dve.wait_ge(s_edges, 16 * 6)
            dve.wait_ge(s_prev, 32)
            dve.wait_ge(s_pc, 1)
            srcf, dstf = flts[:, 0, :, :], flts[:, 1, :, :]
            for k, n in ((0, 128), (1, GL)):
                dve.tensor_copy(srcf[0:n, k, :], ints[0:n, 0, k, :])
                link(dve.tensor_copy(dstf[0:n, k, :], ints[0:n, 1, k, :]))
                for a, b, size in ((hi, srcf, TR), (wd, dstf, WIN)):
                    link(dve.tensor_scalar(a[0:n, k, :], b[0:n, k, :], (size - 1) / 2, 1.0 / size,
                                           ALU.subtract, ALU.mult))
                    link(dve.tensor_scalar(a[0:n, k, :], a[0:n, k, :], ROUND, None, ALU.add))
                    link(dve.tensor_scalar(a[0:n, k, :], a[0:n, k, :], ROUND, None, ALU.subtract))
                link(dve.scalar_tensor_tensor(q16[0:n, 1, k, :], hi[0:n, k, :], -float(TR), srcf[0:n, k, :],
                                              ALU.mult, ALU.add))
                link(dve.scalar_tensor_tensor(dstf[0:n, k, :], wd[0:n, k, :], -float(WIN), dstf[0:n, k, :],
                                              ALU.mult, ALU.add))
                link(dve.scalar_tensor_tensor(q16[0:n, 0, k, :], hi[0:n, k, :], float(WIN), dstf[0:n, k, :],
                                              ALU.mult, ALU.add))
                link(dve.tensor_copy(q16[0:n, 2, k, :], wd[0:n, k, :]))
                link(dve.tensor_tensor(gend[0:n, k:k + 1], wd[0:n, k, GE - 1:GE], gidx[0:n, k:k + 1], ALU.add))
                link(dve.tensor_copy(gprev[0:n, k:k + 1], lastd[0:n, k:k + 1]))
                link(dve.tensor_scalar(gprev[0:n, k:k + 1], gprev[0:n, k:k + 1], (WIN - 1) / 2, 1.0 / WIN,
                                       ALU.subtract, ALU.mult))
                link(dve.tensor_scalar(gprev[0:n, k:k + 1], gprev[0:n, k:k + 1], ROUND, None, ALU.add))
                link(dve.tensor_scalar(gprev[0:n, k:k + 1], gprev[0:n, k:k + 1], ROUND, None, ALU.subtract))
                link(dve.scalar_tensor_tensor(gprev[0:n, k:k + 1], gprev[0:n, k:k + 1], -1.0,
                                              gidx[0:n, k:k + 1], ALU.add, ALU.add))
                link(dve.tensor_scalar(tmpk[0:n, :], iota_s[0:n, :], gprev[0:n, k:k + 1], None, ALU.is_gt))
                link(dve.scalar_tensor_tensor(grouphot[0:n, k, :], iota_s[0:n, :], gend[0:n, k:k + 1],
                                              tmpk[0:n, :], ALU.is_le, ALU.mult))
                dve.tensor_scalar(gcol16[0:n, k, :], iota_s[0:n, 0:128], 0.0, gidx[0:n, k:k + 1],
                                  ALU.mult, ALU.add).then_inc(s_v, 1)
                done[0] += 1
            dve.tensor_copy(ident16[:, :], ident[:, 0:TR]).then_inc(s_diag, 1)
            dve.wait_ge(s_sel, 1)
            link(dve.scalar_tensor_tensor(bstep, P[:, 6, 0:NS], -1.0, iota_s, ALU.mult, ALU.add))
            link(dve.tensor_scalar(steps_off[0:1, :], bstep[0:1, :], float(WIN), None, ALU.mult))
            for h in range(2):
                link(dve.tensor_tensor(tmpk, bstep, P[:, 4 + h, 0:NS], ALU.is_equal))
                link(dve.scalar_tensor_tensor(steptab[:, 0, h, 0:NS], P[:, h, 0:NS], 1.0, tmpk,
                                              ALU.add, ALU.mult))
                link(dve.tensor_copy(steptab[:, 1, h, 0:NS], P[:, 2 + h, 0:NS]))
            dve.sem_inc(s_tab, 1)

            def keyhots(s, slot):
                for h in range(2):
                    last = dve.tensor_scalar(keyhot[:, slot, h, :], iota_key,
                                             steptab[:, 0, h, bass.ds(s, 1)], None, ALU.is_equal)
                last.then_inc(s_key, 1)

            for s in range(AHEAD):
                keyhots(s, s)
            dve.wait_ge(s_zero, 2)
            dve.sem_inc(s_add, 1)
            with dve.Fori(0, NS // UNROLL) as turn:
                s = turn * UNROLL
                _, cols = nc.values_load_multi_w_load_instructions(
                    steps_off[0:1, bass.ds(s, UNROLL)], engines=[mybir.EngineType.DVE],
                    min_val=0, max_val=WIN * (NW - 1),
                    skip_runtime_bounds_check_because="windows are numbered 0 to NW - 1")
                for u in range(UNROLL):
                    keyhots(s + u + AHEAD, (u + AHEAD) % RING)
                    dve.wait_ge(s_cp, s + u + 1)
                    dve.wait_ge(s_add, s + u + 1)
                    place = ATt[0:TR, :, bass.ds(cols[u], WIN)]
                    dve.tensor_tensor(place, place, counted[0:TR, u % RING, :]
                                      .rearrange("p (t c) -> p t c", c=WIN), ALU.add).then_inc(s_add, 1)

            def diagonal(op, s_done):
                step = AC + TR
                d = AT[0:TR, 0:(NT - 1) * step].rearrange("p (t c) -> p t c", c=step)[:, :, 0:TR]
                dve.tensor_tensor(d, d, ident16[0:TR, :].unsqueeze(1).broadcast_to([TR, NT - 1, TR]), op)
                d = AT[0:TR, (NT - 1) * step:(NT - 1) * step + TR]
                dve.tensor_tensor(d, d, ident16[0:TR, :], op).then_inc(s_done, 1)

            dve.wait_ge(s_add, NS + 1)
            diagonal(ALU.add, s_diag)
            dve.wait_ge(s_dcol, 1)
            link(dve.tensor_copy(deg, P[0:TR, 2, 0:NT]))
            dve.sem_inc(s_degc, 1)
            link(dve.reciprocal(rdeg, deg))
            link(dve.tensor_scalar(rneigh, deg, -1.0, 1.0, ALU.add, ALU.max))
            link(dve.reciprocal(rneigh, rneigh))
            dve.wait_ge(s_pow, 1)
            dve.sem_inc(s_rd, 1)

            for t in range(NT):
                dve.wait_ge(s_xh, t + 1)
                dve.scalar_tensor_tensor(Xt[0:TR, t, 1, :], St[0:TR, t % 8, :], dinv[:, t:t + 1],
                                         Xt[0:TR, t, 0, :], ALU.mult, ALU.subtract).then_inc(s_x1, 1)

            def diagonals(i):
                t0, nt = chunk(i)
                for j in range(nt):
                    last = dve.tensor_scalar(DGt[0:TR, j, :], ident[0:TR, 0:TR], sdeg[:, bass.ds(t0 + j, 1)],
                                             None, ALU.mult)
                last.then_inc(s_dg, 1)

            def low_parts(i, l):
                t0, nt = chunk(i)
                for j in range(nt):
                    if j % 2 == 0:
                        dve.wait_ge(s_ph, NT * l + first_of(i) + min(j + 2, nt))
                    dve.scalar_tensor_tensor(parts_out[0:TR, j, 1, :],
                                             P[0:TR, 6 + j // 2, (j % 2) * D:(j % 2 + 1) * D],
                                             rdeg[:, bass.ds(t0 + j, 1)], parts_out[0:TR, j, 0, :],
                                             ALU.mult, ALU.subtract).then_inc(s_pl, 1)

            def layer1(i, k):
                nt = chunk(i)[1]
                if k:
                    dve.wait_ge(s_w1, i)
                diagonals(i)
                dve.wait_ge(s_w1, i + 1)
                if k:
                    dve.wait_ge(s_wx, i)
                dve.tensor_scalar(hT[:, :, 0:nt * TR], P[:, 4:6, 0:nt * TR], 0.0, None, ALU.max).then_inc(s_h, 1)
                low_parts(i, 0)

            chunks(dve, layer1)

            def layer2(i, k):
                nt = chunk(i)[1]
                if k:
                    dve.wait_ge(s_used, NC * (NC + i))
                diagonals(i)
                dve.wait_ge(s_used, NC * (NC + i + 1))
                dve.wait_ge(s_wx, NC + i)
                b = 2 * ((NC + k) % 2)
                dve.tensor_scalar(hT[:, :, 0:nt * TR], P[:, b:b + 2, 0:nt * TR], 0.0, None, ALU.max
                                  ).then_inc(s_h, 1)
                low_parts(i, 1)

            chunks(dve, layer2)

            def normalise(i, k, li, bank, scale, count):
                t0, nt = chunk(i)
                base = done[0]
                for j in range(nt):
                    last = dve.scalar_tensor_tensor(ring_tile(k, j),
                                                    P[0:TR, bank + j // 2, (j % 2) * D:(j % 2 + 1) * D],
                                                    scale[:, bass.ds(t0 + j, 1)], ring_tile(k, j),
                                                    ALU.mult, ALU.add)
                last.then_inc(s_aev, 1)
                dve.wait_ge(s_aev, NC + li + 1)
                for j in range(nt):
                    last = dve.bn_stats(stats[0:TR, j, :], ring_tile(k, j))
                last.then_inc(s_v, 1)
                dve.wait_ge(s_v, base + li + 1)
                dve.nop(nofuse=True)
                for j in range(nt):
                    last = dve.bn_aggr(mv[0:TR, j, :], stats[0:TR, j, :])
                last.then_inc(s_mv, 1)
                dve.wait_ge(s_rs, li + 1)
                dve.wait_ge(s_mv, li + 1)
                for j in range(nt):
                    dve.tensor_scalar(ring_tile(k, j), ring_tile(k, j), mv[0:TR, j, 0:1], rstd[0:TR, j:j + 1],
                                      ALU.subtract, ALU.mult).then_inc(s_ln, 1)

            rounds = TOPK // 8
            s_top = s_topk

            def layer3(i, k):
                t0, nt = chunk(i)
                dve.wait_ge(s_used, NC * (2 * NC + i + 1))
                dve.wait_ge(s_xb, i + 1)
                normalise(i, k, i, 2 * ((2 * NC + k) % 2), dinv, 0)
                for j in range(nt):
                    o = first_of(i) + j
                    dve.wait_ge(s_hh, o + 1)
                    dve.tensor_tensor(ring_tile(k, j), ring_tile(k, j), P[0:TR, 6 + slot2(k, j), 0:D], ALU.add
                                      ).then_inc(s_bs, 1)
                    dve.wait_ge(s_hn, o + 1)
                    dve.nop(nofuse=True)
                    n = (2 * rounds) * o
                    row = neigh_row
                    for r in range(rounds):
                        dve.max(top8[0:TR, r, :], row).then_inc(s_top, 1)
                        dve.wait_ge(s_top, n + 2 * r + 1)
                        dve.nop(nofuse=True)
                        dve.match_replace(neigh_left, top8[0:TR, r, :], row, GONE).then_inc(s_top, 1)
                        dve.wait_ge(s_top, n + 2 * r + 2)
                        dve.nop(nofuse=True)
                        row = neigh_left
                    dve.wait_ge(s_pl, 2 * NT + o)
                    dve.scalar_tensor_tensor(sparse_row, neigh_left, GONE, neigh_row, ALU.is_le, ALU.mult
                                             ).then_inc(s_sp, 1)

            chunks(dve, layer3)

            dve.wait_ge(s_used, NC * (3 * NC))
            diagonal(ALU.subtract, s_nd)

            def layer4(i, k):
                dve.wait_ge(s_used, NC * (3 * NC + i + 1))
                dve.wait_ge(s_xr[k % 2], 16 * (4 - k % 2) + 8 * (i + 2 - k % 2))
                normalise(i, k, NC + i, 2 * ((3 * NC + k) % 2), rneigh, NT)

            chunks(dve, layer4)

        @block.tensor
        def _(pe):
            pe.wait_ge(s_diag, 1)
            blocks = ((0, 128), (1, GL))
            for q in range(3):
                for h in range(2):
                    for k, n in blocks:
                        pe.matmul(P[:, 2 * q + h, 0:NS], q16[0:n, q, k, 128 * h:128 * h + 128],
                                  grouphot[0:n, k, :], start=k == 0, stop=k == 1)
            for k, n in blocks:
                last = pe.matmul(P[:, 6, 0:NS], gcol16[0:n, k, :], grouphot[0:n, k, :], start=k == 0, stop=k == 1)
            last.then_inc(s_sel, 1)

            pe.wait_ge(s_tab, 1)
            with pe.Fori(0, NS // UNROLL) as turn:
                s = turn * UNROLL
                for u in range(UNROLL):
                    pe.wait_ge(s_key, s + u + 1)
                    pe.wait_ge(s_lo, s + u + 2)
                    for h in range(2):
                        last = pe.matmul(P[0:TR, u % RING, 0:KEYS], lohot[:, u % RING, h, 0:TR],
                                         keyhot[:, u % RING, h, :], start=h == 0, stop=h == 1)
                    last.then_inc(s_cnt, 1)

            pe.wait_ge(s_diag, 2)
            for c in range(NXG):
                n = min(CW, N - CW * c)
                if c >= 2:
                    pe.wait_ge(s_dcp, c - 1)
                for t in range(NT):
                    last = pe.matmul(P[0:1, c % 2, 0:n], one16[0:TR, :], ATt[0:TR, t, CW * c:CW * c + n],
                                     start=t == 0, stop=t == NT - 1)
                last.then_inc(s_drow, 1)
                pe.wait_ge(s_dcp, c + 1)
                for j in range(n // TR):
                    col = 8 * D + 512 * (c % 2) + j * TR
                    last = pe.matmul(P[0:TR, 2, CT * c + j:CT * c + j + 1], S[0:1, col:col + TR],
                                     one32[0:1, 0:1], start=True, stop=True)
            last.then_inc(s_dcol, 1)

            def agg_group(k, l, t0, nt, tile, n, first, final):
                if first and l >= 2:
                    for j in range(0, nt, 2):
                        w = min(2, nt - j) * D
                        pe.matmul(P[0:TR, 2 * (k % 2) + j // 2, 0:w], zero16[0:TR, :], AT[0:TR, 0:w],
                                  start=True, stop=False)
                for u in range(n):
                    t = tile + u
                    if l < 2:
                        rhs = AT[0:TR, bass.ds(t * AC + t0 * TR, nt * TR)]
                        for h in range(2):
                            for a in range(2):
                                lhs = X[0:TR, bass.ds(t * 2 * D + a * D + h * 128, 128)]
                                last = pe.matmul(P[:, 2 * (k % 2) + h, 0:nt * TR], lhs, rhs,
                                                 start=first and u == 0 and a == 0,
                                                 stop=final and u == n - 1 and a == 1)
                    else:
                        for j in range(nt):
                            lhs = AT[0:TR, bass.ds(t * AC + (t0 + j) * TR, TR)]
                            for a in range(2):
                                rhs = X[0:TR, bass.ds(t * 2 * D + a * D, D)]
                                last = pe.matmul(P[0:TR, 2 * (k % 2) + j // 2, (j % 2) * D:(j % 2 + 1) * D],
                                                 lhs, rhs, start=False,
                                                 stop=final and u == n - 1 and a == 1
                                                 and (j % 2 == 1 or j == nt - 1))
                return last

            def aggregate(i, k, l, between):
                t0, nt = chunk(i)
                kk = NC * l + k
                for q in range(NC):
                    if k == 0 and l == 0:
                        pe.wait_ge(s_x1, 4 * q + 1)
                    elif k == 0:
                        pe.wait_ge(s_re[q], 16 * l)
                    last = agg_group(kk, l, t0, nt, 0 if q == 0 else 4 * q - 3, 1 if q == 0 else CT,
                                     q == 0, q == NC - 1)
                    last.then_inc(s_used, 1)
                    between(q)

            def diag_bias(bank, l, nt):
                for h in range(2):
                    for j in range(nt):
                        pe.matmul(P[:, bank + h, j * TR:(j + 1) * TR], B12[0:TR, l, 128 * h:128 * h + 128],
                                  DGt[0:TR, j, :], start=False, stop=False)

            def apply_w1(i):
                t0, nt = chunk(i)
                pe.wait_ge(s_aev, i + 1)
                pe.wait_ge(s_dg, i + 1)
                for kt in range(2):
                    for h in range(2):
                        last = pe.matmul(P[:, 4 + h, 0:nt * TR], W[:, kt, 128 * h:128 * h + 128],
                                         aggT[:, kt, 0:nt * TR], start=kt == 0, stop=kt == 1)
                    if kt == 0:
                        diag_bias(4, 0, nt)
                last.then_inc(s_w1, 1)

            def next_operand(i, l):
                nt = chunk(i)[1]
                pe.wait_ge(s_h, NC * l + i + 1)
                if not (isinstance(i, int) and i == 0 and l == 0):
                    pe.wait_ge(s_pl, NT * l + first_of(i))
                for j in range(nt):
                    for kt in range(2):
                        w = W[:, kt, D:2 * D] if l == 0 else W3[:, kt, :]
                        last = pe.matmul(P[0:TR, 6 + j // 2, (j % 2) * D:(j % 2 + 1) * D],
                                         hT[:, kt, j * TR:(j + 1) * TR], w, start=kt == 0, stop=kt == 1)
                last.then_inc(s_wx, 1)

            pe.wait_ge(s_wts, 16 * 6)

            def layer1(i, k):
                def between(q):
                    if k and q == 2:
                        apply_w1(i - 1)
                    if k and q == 5:
                        next_operand(i - 1, 0)
                if k >= 2:
                    pe.wait_ge(s_aev, i - 1)
                aggregate(i, k, 0, between)

            chunks(pe, layer1)
            apply_w1(NC - 1)
            next_operand(NC - 1, 0)

            def layer2(i, k):
                def between(q):
                    if k and q == 3:
                        next_operand(i - 1, 1)
                    if q == 5:
                        pe.wait_ge(s_dg, NC + i + 1)
                        diag_bias(2 * ((NC + k) % 2), 1, chunk(i)[1])
                pe.wait_ge(*((s_aev, 6 + i) if k < 2 else (s_h, NC + i - 1)))
                aggregate(i, k, 1, between)

            chunks(pe, layer2)
            next_operand(NC - 1, 1)

            def transpose_x1(i, k, j):
                o = first_of(i) + j
                pe.wait_ge(s_ln, o + 1)
                if k or j >= 2:
                    pe.wait_ge(s_tc, o - 1)
                for h in range(2):
                    last = pe.transpose(P[:, 4 + slot2(k, j), h * TR:(h + 1) * TR],
                                        ring_tile(k, j)[:, 128 * h:128 * h + 128], ident[0:TR, 0:TR])
                last.then_inc(s_tr, 1)

            def self_and_neighbour(i, k, j):
                o = first_of(i) + j
                pe.wait_ge(s_tc, o + 1)
                if k or j >= 2:
                    pe.wait_ge(s_bs, o - 1)
                    pe.wait_ge(s_hn, o - 1)
                for h in range(2):
                    last = pe.matmul(P[0:TR, 6 + slot2(k, j), :], x1T[slot2(k, j)][:, h, :], W[:, h, :],
                                     start=h == 0, stop=h == 1)
                last.then_inc(s_hh, 1)

            def tile_work(i, k, q):
                nt = chunk(i)[1]
                if 1 <= q <= nt:
                    transpose_x1(i, k, q - 1)
                if 2 <= q <= nt + 1:
                    self_and_neighbour(i, k, q - 2)

            def layer3(i, k):
                pe.wait_ge(*((s_h, 2 * NC - 1 + i) if k < 2 else (s_aev, NC + i - 1)))
                prev = {1: 0, 2: 1, 3: 2, 4: 3}
                aggregate(i, k, 2, (lambda q: tile_work(i - 1, prev[k], q)) if k else (lambda q: None))

            pe.wait_ge(s_wn, 32)
            chunks(pe, layer3)
            for q in range(1, CT + 2):
                tile_work(NC - 1, 4, q)

            pe.wait_ge(s_nd, 1)

            def layer4(i, k):
                pe.wait_ge(s_aev, 2 * NC + i - 1)
                aggregate(i, k, 3, lambda q: None)

            chunks(pe, layer4)


def kernel(x, src, dst, L0_gnn_W1, L0_gnn_b1, L0_gnn_W2, L0_gnn_b2, L0_gnn_W3, L0_gnn_b3, L1_gnn_W_self,
           L1_gnn_W_neigh):
    import concourse.bacc as bacc
    from concourse.bass_utils import run_bass_kernel_spmd as run

    nc = bacc.Bacc("TRN2", target_bir_lowering=False, num_devices=1)
    arrays, args = {}, []
    given = [("x", x), ("src", src), ("dst", dst), ("w1", L0_gnn_W1), ("b1", L0_gnn_b1), ("w2", L0_gnn_W2),
             ("b2", L0_gnn_b2), ("w3", L0_gnn_W3), ("b3", L0_gnn_b3), ("wself", L1_gnn_W_self),
             ("wneigh", L1_gnn_W_neigh)]
    for name, a in given:
        a = np.ascontiguousarray(a)
        arrays[f"in_{name}"] = a
        args.append(nc.dram_tensor(f"in_{name}", a.shape, mybir.dt.from_np(a.dtype), kind="ExternalInput").ap())
    args.append(nc.dram_tensor("out", (N, D), F32, kind="ExternalOutput").ap())
    gnn(nc, *args)
    r = run(nc, [arrays], core_ids=[0])
    return r.results[0]["out"]
```

```python
import numpy as np
import concourse.bass as bass
from concourse import mybir
from concourse.alu_op_type import AluOpType as ALU

F32 = mybir.dt.float32
F16 = mybir.dt.float16
I32 = mybir.dt.int32
ACT = mybir.ActivationFunctionType

N = 3125
E = 50000
D = 256
TR = 125
NT = N // TR
HB = D // 128

WIN = 20
NW = -(-N // WIN)
AC = NW * WIN
GE = 128
NG = -(-E // GE)
GK = -(-NG // 128)
GL = NG - 128 * (GK - 1)
ELAST = E - GE * (NG - 1)
UNROLL = 28
NS = -(-(NW + NG - 1) // UNROLL) * UNROLL
AHEAD = 3
RING = AHEAD + 1
NSP = NS + RING
LORING = UNROLL // 2
NOWHERE = 40000
ROUND = 1.5 * 2 ** 23

CT = 4
CW = CT * TR
NC = 1 + (NT - 1) // CT
FIRST = 8
TOPK = 32
ZERO_SPLIT = NT * AC // 20 * 8
GONE = -3.0e38


def chunk(i):
    if isinstance(i, int) and i < 2:
        return (1, CT) if i == 0 else (0, 1)
    return CT * i - (CT - 1), CT


def first_of(i):
    if isinstance(i, int) and i < 2:
        return CT * i
    return CT * i - (CT - 1)


def gnn(nc, x, src, dst, w1, b1, w2, b2, w3, b3, wself, wneigh, out):
    def sb(name, shape, dt):
        return nc.alloc_sbuf_tensor(name, shape, dt).ap()

    def sem(name):
        return nc.alloc_semaphore(name)

    xparts_dram = [nc.dram_tensor(f"xparts{l}", (NT, TR, 2 * D), F16, kind="Internal").ap() for l in range(3)]
    base_dram = nc.dram_tensor("base", (NT, TR, D), F32, kind="Internal").ap()

    AT = sb("AT", [128, NT * AC], F16)
    X = sb("X", [128, NT * 2 * D], F16)
    S = sb("S", [128, 14 * D], F32)
    W = sb("W", [128, HB, 2 * D], F32)
    W3 = sb("W3", [128, HB, D], F32)
    DG = sb("DG", [128, CT * TR], F32)
    B12 = sb("B12", [128, 2, D], F32)
    B3 = sb("B3", [128, D], F32)
    ident = sb("ident", [128, 128], F32)
    ident16 = sb("ident16", [128, TR], F16)
    zero16 = sb("zero16", [128, TR], F16)
    minus16 = sb("minus16", [128, TR], F16)
    one16 = sb("one16", [128, 32], F16)
    zero32 = sb("zero32", [128, 1], F32)
    tabs = sb("tabs", [128, 8, NT], F32)
    deg, dinv, sdeg, rdeg, rneigh = (tabs[0:TR, i, :] for i in range(5))
    mhalf = tabs[0:TR, 5, :]
    steps_off = sb("steps_off", [1, NS], I32)
    stats = sb("stats", [128, CT, 6], F32)
    mv = sb("mv", [128, CT, 2], F32)
    rstd = sb("rstd", [128, CT], F32)
    ATt = AT.rearrange("p (t c) -> p t c", t=NT)
    Xt = X.rearrange("p (t a d) -> p t a d", t=NT, a=2)
    St = S.rearrange("p (k d) -> p k d", d=D)
    cols = St[0:TR, 12, 0:128]
    sdT16 = St[:, 12, 128:192].bitcast(F16)[:, 0:TR]
    sd16 = St[0:TR, 12, 192:192 + NT].bitcast(F16).rearrange("p (a t) -> p a t", a=2)
    blocksel = St[:, 12, 224:224 + NT]
    BR = St[:, 13, :].bitcast(F16).rearrange("p (l d) -> p l d", l=2)
    top8 = B12[:, 0, 0:2 * TOPK].rearrange("p (v r e) -> p v r e", v=2, e=8)
    DG16 = DG[:, 0:CT * TR // 2].bitcast(F16)
    DGt = DG16.rearrange("p (j n) -> p j n", j=CT)

    KEYS = NT * WIN
    o = 0
    keyhot = X[:, o:o + RING * KEYS].rearrange("p (r n) -> p r n", r=RING)
    o += RING * KEYS
    counted = X[:, o:o + RING * KEYS].rearrange("p (r n) -> p r n", r=RING)
    o += RING * KEYS
    GX = GK * GE
    hi = X[:, o:o + 2 * GX].bitcast(F32)
    o += 2 * GX
    wd = X[:, o:o + 2 * GX].bitcast(F32)
    lohot = X[:, o - 2 * GX:o - 2 * GX + LORING * 128].rearrange("p (r n) -> p r n", r=LORING)
    assert LORING * 128 <= 4 * GX
    o += 2 * GX
    q16 = X[:, o:o + 3 * GX].rearrange("p (q k e) -> p q k e", q=3, k=GK)
    o += 3 * GX
    gcol16 = X[:, o:o + GX].rearrange("p (k m) -> p k m", k=GK)
    o += GX
    grouphot = X[:, o:o + GK * NS].rearrange("p (k s) -> p k s", k=GK)
    o += GK * NS
    iota_key = X[:, o:o + KEYS]
    o += KEYS
    iota_lo = X[:, o:o + 126]
    o += 126
    sums = X[0:3 * NT, NT * 2 * D - N:]
    assert o <= NT * 2 * D, o

    o = 0
    steptab = S[:, o:o + 2 * NSP].rearrange("p (q s) -> p q s", q=2)
    o += 2 * NSP
    iota_s = S[:, o:o + NS]
    o += NS
    turn_lo = S[:, o:o + UNROLL]
    o += UNROLL
    gend = S[:, o:o + GK]
    o += GK
    gprev = S[:, o:o + GK]
    o += GK
    gidx = S[:, o:o + GK]
    o += GK
    lastd = S[:, o:o + GK].bitcast(I32)
    o += GK
    bstep = S[:, o:o + NS]
    tmpk = S[:, o + NS:o + 2 * NS]
    ints = S[:, o:o + 2 * GX].bitcast(I32).rearrange("p (q e) -> p q e", q=2)
    flts = S[:, o:o + 2 * GX].rearrange("p (q e) -> p q e", q=2)
    o += max(2 * NS, 2 * GX)
    assert o <= 14 * D, o
    SH = NS // 2

    P = nc.alloc_psum_tensor("P", [128, 8, 512], F32).ap()

    s_edges = sem("edges_loaded")
    s_prev = sem("previous_dst_loaded")
    s_wts = sem("weights_loaded")
    s_pc = sem("pool_constants_ready")
    s_dc = sem("dve_constants_ready")
    s_v = sem("dve_step_done")
    s_p = sem("pool_step_done")
    s_zero = sem("at_zeroed")
    s_sel = sem("edges_selected")
    s_tab = sem("step_tables_ready")
    s_key = sem("keyhot_ready")
    s_lo = sem("lohot_ready")
    s_turn = sem("turn_columns_copied")
    s_cnt = sem("window_counted")
    s_cp = sem("counted_copied")
    s_add = sem("counted_added")
    s_diag = sem("self_loops_added")
    s_sums = sem("source_tile_sums_moved")
    s_dcol = sem("degree_columns_ready")
    s_degc = sem("degrees_copied")
    s_sdc = sem("sqrt_degree_columns_ready")
    s_sdt = sem("sqrt_degrees_transposed")
    s_pow = sem("degree_powers_ready")
    s_rd = sem("degree_tables_ready")
    s_xl = [sem(f"x_loaded{i}") for i in range(2)]
    s_xh = sem("x1_high_ready")
    s_x1 = sem("x1_parts_ready")
    s_aev = sem("chunk_evacuated")
    s_dg = sem("diagonals_ready")
    s_w1 = sem("w1_applied")
    s_h = sem("hidden_ready")
    s_wx = sem("next_operand_multiplied")
    s_ph = sem("high_parts_ready")
    s_pl = sem("low_parts_ready")
    s_st = sem("parts_stored")
    s_st3 = [sem(f"last_parts_stored{i}") for i in range(2)]
    s_used = sem("operand_tiles_used")
    s_re = [sem(f"operand_reloaded{i}") for i in range(NC)]
    s_xr = [sem(f"residual_loaded{i}") for i in range(2)]
    s_xb = sem("residual_and_bias_ready")
    s_mv = sem("mean_and_variance_ready")
    s_rs = sem("rstd_ready")
    s_ln = sem("normalised")
    s_tr = sem("x1_transposed")
    s_tc = sem("x1_transpose_copied")
    s_hh = sem("self_and_neighbour_ready")
    s_hn = sem("neighbour_copied")
    s_bs = sem("base_ready")
    s_bst = [sem(f"base_stored{i}") for i in range(2)]
    s_sp = sem("sparse_ready")
    s_wn = sem("neighbour_weights_loaded")
    s_topk = sem("topk_step_done")
    s_out = [sem(f"out_stored{i}") for i in range(2)]

    AT1 = [ATt[TR + c:TR + c + 1, :, 0:N] for c in range(3)]

    def parts_rows(l, t0, nt):
        return xparts_dram[l][bass.ds(t0, nt), :, :].rearrange("t p e -> p t e")

    def tile_rows(a, t0, nt):
        return a[bass.ds(t0, nt), :, :].rearrange("t p d -> p t d")

    x_t = x.rearrange("(t p) d -> t p d", p=TR)
    out_t = out.rearrange("(t p) d -> t p d", p=TR)
    parts_out = S[:, 8 * D:12 * D].bitcast(F16).rearrange("p (j a d) -> p j a d", j=CT, a=2)
    aggT = St[:, 0:4, :].rearrange("p k d -> p (k d)")[:, 0:2 * CW].rearrange("p (h n) -> p h n", h=2)
    hT = St[:, 4:8, :].rearrange("p k d -> p (k d)")[:, 0:2 * CW].rearrange("p (h n) -> p h n", h=2)
    NXG = -(-NT // 4)

    def chunks(eng, step):
        for i in range(3):
            step(i, i)
        with eng.Fori(0, (NC - 3) // 2) as turn:
            step(2 * turn + 3, 3)
            step(2 * turn + 4, 4)

    def slot2(k, j):
        return (first_of(k) + j) % 2

    def ring_slots(k, nt):
        return St[0:TR, 4 * (k % 2):4 * (k % 2) + nt, :]

    def ring_tile(k, j):
        return St[0:TR, 4 * (k % 2) + j, :]

    last_parts = [St[0:TR, 8 + r, :].bitcast(F16).rearrange("p (a d) -> p a d", a=2) for r in range(2)]
    neigh_row = [St[0:TR, 10, :], St[0:TR, 13, :]]
    neigh_left = [St[0:TR, 11, :], St[0:TR, 12, :]]
    x1T = [DG[:, r * 2 * TR:(r + 1) * 2 * TR].rearrange("p (h n) -> p h n", h=2) for r in range(2)]

    def agg_bank(li, h):
        return P[:, 2 * (li % 2) + h, :]

    with nc.Block() as block:

        @block.sync
        def _(sp):
            sp.wait_ge(s_dc, 1)
            full = 128 * (GK - 1)
            for q, a in ((0, src), (1, dst)):
                sp.dma_start(ints[:, q, 0:(GK - 1) * GE].rearrange("p (k e) -> p k e", e=GE),
                             a[0:full * GE].rearrange("(k p e) -> p k e", p=128, e=GE)).then_inc(s_edges, 16)
                sp.dma_start(ints[0:GL - 1, q, (GK - 1) * GE:],
                             a[full * GE:(NG - 1) * GE].rearrange("(g e) -> g e", e=GE)).then_inc(s_edges, 16)
                sp.dma_start(ints[GL - 1:GL, q, (GK - 1) * GE:(GK - 1) * GE + ELAST],
                             a[GE * (NG - 1):E].rearrange("(g e) -> g e", g=1)).then_inc(s_edges, 16)
            last = dst[0:(NG - 1) * GE].rearrange("(g e) -> g e", e=GE)[:, GE - 1:GE]
            sp.dma_start(lastd[1:128, 0:1], last[0:127, :], allow_slow_non_contiguous=True).then_inc(s_prev, 16)
            for k in range(1, GK):
                n = min(128, NG - 128 * k)
                sp.dma_start(lastd[0:n, k:k + 1], last[128 * k - 1:128 * k - 1 + n, :],
                             allow_slow_non_contiguous=True).then_inc(s_prev, 16)
            for a, dest in ((w1, W[:, :, 0:D]), (w2, W[:, :, D:2 * D]), (w3, W3[:, :, :])):
                sp.dma_start(dest, a.rearrange("(h p) d -> p h d", p=128)).then_inc(s_wts, 16)
            for a, dest in ((b1, B12[:, 0, :]), (b2, B12[:, 1, :]), (b3, B3[:, :])):
                sp.dma_start(dest, a.rearrange("(o d) -> o d", o=1).broadcast_to([128, D])).then_inc(s_wts, 16)
            sp.wait_ge(s_add, NS + 1)
            for c in range(3):
                sp.dma_start(sums[c * NT:(c + 1) * NT, :], AT1[c]).then_inc(s_sums, 16)
            for g in range(NXG):
                nt = min(4, NT - 4 * g)
                if g >= 2:
                    sp.wait_ge(s_x1, 4 * (g - 1))
                sp.dma_start(St[0:TR, 4 * (g % 2):4 * (g % 2) + nt, :],
                             tile_rows(x_t, 4 * g, nt)).then_inc(s_xl[g % 2], 16)

            def reload(l, groups):
                for q in groups:
                    t0, nt = (0, 1) if q == 0 else (4 * q - 3, CT)
                    i = {0: 1, 1: 0}.get(q, q)
                    if l < 2:
                        sp.wait_ge(s_st, 16 * (NC * l + max(i + 1, 2 if q < 2 else 0)))
                    else:
                        done = first_of(i) + nt
                        sp.wait_ge(s_st3[0], 16 * ((done + 1) // 2))
                        sp.wait_ge(s_st3[1], 16 * (done // 2))
                    sp.wait_ge(s_used, NC * NC * l + NC * (NC - 1) + q + 1)
                    sp.dma_start(Xt[0:TR, t0:t0 + nt, :, :].rearrange("p t a d -> p t (a d)"),
                                 parts_rows(l, t0, nt)).then_inc(s_re[q], 16)

            for l in range(2):
                for i in range(NC):
                    t0, nt = chunk(i)
                    if i == NC - 1:
                        reload(l, range(NC - 1))
                    sp.wait_ge(s_ph, NT * l + first_of(i) + nt)
                    sp.wait_ge(s_pl, NT * l + first_of(i) + nt)
                    sp.dma_start(parts_rows(l, t0, nt),
                                 parts_out[0:TR, 0:nt, :, :].rearrange("p j a d -> p j (a d)")).then_inc(s_st, 16)
                    if l == 0 and i == NC - 1:
                        sp.wait_ge(s_wx, NC)
                        for a, dest in ((wself, W[:, :, 0:D]), (wneigh, W[:, :, D:2 * D])):
                            sp.dma_start(dest, a.rearrange("(h p) d -> p h d", p=128)).then_inc(s_wn, 16)
                reload(l, [NC - 1])

            def load_ring(i, rows):
                t0, nt = chunk(i)
                sp.dma_start(ring_slots(i, nt), tile_rows(rows, t0, nt)).then_inc(s_xr[i % 2], 16)

            sp.wait_ge(s_wx, 2 * NC)
            load_ring(0, x_t)
            load_ring(1, x_t)
            for i in range(NC):
                t0, nt = chunk(i)
                if i == NC - 1:
                    reload(2, range(NC - 1))
                for j in range(nt):
                    o = first_of(i) + j
                    sp.wait_ge(s_bs, o + 1)
                    sp.dma_start(tile_rows(base_dram, t0 + j, 1), ring_slots(i, nt)[:, j:j + 1, :]
                                 ).then_inc(s_bst[i % 2], 16)
                    sp.wait_ge(s_ph, 2 * NT + o + 1)
                    sp.wait_ge(s_pl, 2 * NT + o + 1)
                    sp.dma_start(parts_rows(2, t0 + j, 1), last_parts[o % 2].rearrange("p a d -> p (a d)")
                                 .unsqueeze(1)).then_inc(s_st3[o % 2], 16)
                if i + 2 < NC:
                    sp.wait_ge(s_bst[i % 2], 16 * sum(chunk(c)[1] for c in range(i % 2, i + 1, 2)))
                    load_ring(i + 2, x_t)
            reload(2, [NC - 1])

            for r in range(2):
                sp.wait_ge(s_bst[r], 16 * sum(chunk(c)[1] for c in range(r, NC, 2)))
            load_ring(0, base_dram)
            load_ring(1, base_dram)
            for i in range(NC):
                t0, nt = chunk(i)
                sp.wait_ge(s_ln, NT + first_of(i) + nt)
                sp.dma_start(tile_rows(out_t, t0, nt), ring_slots(i, nt)).then_inc(s_out[i % 2], 16)
                if i + 2 < NC:
                    sp.wait_ge(s_out[i % 2], 16 * (i // 2 + 1))
                    load_ring(i + 2, base_dram)
            for r in range(2):
                sp.wait_ge(s_out[r], 16 * len(range(r, NC, 2)))

        @block.gpsimd
        def _(pool):
            done = [0]

            def link(ins):
                done[0] += 1
                ins.then_inc(s_p, 1)
                pool.wait_ge(s_p, done[0])

            link(pool.memset(ident[:, :], 0.0))
            link(pool.affine_select(out=ident[:, :], in_=ident[:, :], compare_op=ALU.not_equal, fill=1.0,
                                    base=0, pattern=[[-1, 128]], channel_multiplier=1))
            link(pool.iota(iota_s, pattern=[[1, NS]], base=0, channel_multiplier=0,
                           allow_small_or_imprecise_dtypes=True))
            link(pool.iota(gidx, pattern=[[128, GK]], base=0, channel_multiplier=1,
                           allow_small_or_imprecise_dtypes=True))
            link(pool.iota(iota_key, pattern=[[1, KEYS]], base=1, channel_multiplier=0,
                           allow_small_or_imprecise_dtypes=True))
            pool.iota(iota_lo, pattern=[[1, 126]], base=0, channel_multiplier=0,
                      allow_small_or_imprecise_dtypes=True).then_inc(s_pc, 1)
            pool.memset(AT[:, 0:ZERO_SPLIT].bitcast(F32), 0.0).then_inc(s_zero, 1)

            pool.wait_ge(s_tab, 1)
            link(pool.memset(lohot[:, :, TR:128], 0.0))
            for c, (p0, p1) in enumerate(((0, 32), (32, 64), (64, 128))):
                link(pool.memset(lohot[p0:p1, :, TR + c:TR + c + 1], 1.0))
            pool.sem_inc(s_lo, 1)
            with pool.Fori(0, NS // UNROLL) as turn:
                s = turn * UNROLL
                pool.wait_ge(s_lo, s + 1)
                pool.nop(nofuse=True)
                pool.tensor_copy(turn_lo, steptab[:, 1, bass.ds(s, UNROLL)]).then_inc(s_turn, 1)
                pool.wait_ge(s_turn, turn + 1)
                for u in range(UNROLL):
                    pool.wait_ge(s_cnt, s + u + 1)
                    pool.nop(nofuse=True)
                    pool.tensor_scalar(lohot[:, u % LORING, 0:TR], iota_lo[:, 0:TR], turn_lo[:, u:u + 1], None,
                                       ALU.is_equal).then_inc(s_lo, 1)

            pool.wait_ge(s_degc, 1)
            for a, b in ((0, FIRST), (FIRST, NT)):
                pool.tensor_tensor(dinv[:, a:b], deg[:, a:b], mhalf[:, a:b], ALU.pow).then_inc(s_pow, 1)

            def finish_rstd(k, li, nt):
                pool.wait_ge(s_mv, li + 1)
                pool.nop(nofuse=True)
                pool.tensor_scalar(rstd[0:TR, 0:nt], mv[0:TR, 0:nt, 1], 1e-5, None, ALU.add).then_inc(s_p, 1)
                pool.wait_ge(s_p, done[0] + 1 + li)
                pool.tensor_tensor(rstd[0:TR, 0:nt], rstd[0:TR, 0:nt], mhalf[:, 0:nt], ALU.pow).then_inc(s_rs, 1)

            def add_bias(i):
                nt = chunk(i)[1]
                pool.wait_ge(s_xr[i % 2], 16 * (i // 2 + 1))
                pool.tensor_tensor(ring_slots(i, nt), ring_slots(i, nt),
                                   B3[0:TR, :].unsqueeze(1).broadcast_to([TR, nt, D]), ALU.add).then_inc(s_xb, 1)

            pool.wait_ge(s_wts, 16 * 6)
            add_bias(0)
            for i in range(NC):
                finish_rstd(i, i, chunk(i)[1])
                if i + 1 < NC:
                    add_bias(i + 1)
                for j in range(chunk(i)[1]):
                    o = first_of(i) + j
                    pool.wait_ge(s_ph, 2 * NT + o + 1)
                    pool.tensor_tensor(last_parts[o % 2][:, 1, :], neigh_row[o % 2], last_parts[o % 2][:, 0, :],
                                       ALU.subtract).then_inc(s_pl, 1)

            def layer4(i, k):
                finish_rstd(k, NC + i, chunk(i)[1])

            chunks(pool, layer4)

        @block.scalar
        def _(act):
            act.wait_ge(s_dc, 1)
            n = (NT * AC - ZERO_SPLIT) // 2
            act.activation(AT[:, ZERO_SPLIT:].bitcast(F32), zero32[:, :].broadcast_to([128, n]), ACT.Copy
                           ).then_inc(s_zero, 1)
            with act.Fori(0, NS // UNROLL) as turn:
                s = turn * UNROLL
                for u in range(UNROLL):
                    act.wait_ge(s_cnt, LORING + s + u + 1)
                    act.activation(counted[:, u % RING, :], P[:, u % RING, 0:KEYS], ACT.Copy).then_inc(s_cp, 1)

            for t in range(NT):
                act.wait_ge(s_pow, 1 if t < FIRST else 2)
                act.wait_ge(s_xl[t // 4 % 2], 16 * (t // 8 + 1))
                act.activation(Xt[0:TR, t, 0, :], St[0:TR, t % 8, :], ACT.Copy,
                               scale=dinv[:, t:t + 1]).then_inc(s_xh, 1)

            def high_parts(i, k, l):
                t0, nt = chunk(i)
                act.wait_ge(s_wx, NC * l + i + 1)
                if l or k:
                    act.wait_ge(s_st, 16 * (NC * l + i))
                for j in range(nt):
                    act.activation(parts_out[0:TR, j, 0, :], P[0:TR, 6 + j // 2, (j % 2) * D:(j % 2 + 1) * D],
                                   ACT.Copy, scale=rdeg[:, bass.ds(t0 + j, 1)]).then_inc(s_ph, 1)

            def layer1(i, k):
                t0, nt = chunk(i)
                act.wait_ge(s_used, NC * (i + 1))
                if k:
                    act.wait_ge(s_w1, i)
                act.activation(aggT[:, :, 0:nt * TR], P[:, 2 * (k % 2):2 * (k % 2) + 2, 0:nt * TR],
                               ACT.Copy).then_inc(s_aev, 1)
                high_parts(i, k, 0)

            act.wait_ge(s_rd, 1)
            chunks(act, layer1)
            chunks(act, lambda i, k: high_parts(i, k, 1))

            def layer3(i, k):
                nt = chunk(i)[1]

                def copy_transposed(j):
                    o = first_of(i) + j
                    act.wait_ge(s_tr, o + 1)
                    act.activation(x1T[slot2(k, j)], P[:, 4 + slot2(k, j), 0:2 * TR]
                                   .rearrange("p (h n) -> p h n", h=2), ACT.Copy).then_inc(s_tc, 1)

                def copy_neighbour(j):
                    o = first_of(i) + j
                    act.wait_ge(s_bs, o + 1)
                    if k or j >= 2:
                        act.wait_ge(s_pl, 2 * NT + o - 1)
                    act.activation(neigh_row[slot2(k, j)], P[0:TR, 6 + slot2(k, j), D:2 * D], ACT.Copy
                                   ).then_inc(s_hn, 1)

                def high_part(j):
                    o = first_of(i) + j
                    act.wait_ge(s_sp, o + 1)
                    if k >= 3:
                        act.wait_ge(s_st3[slot2(k, j)], 8 * (o - slot2(k, j)))
                    elif o >= 2:
                        act.wait_ge(s_st3[o % 2], 16 * (o // 2))
                    act.activation(last_parts[slot2(k, j)][:, 0, :], neigh_row[slot2(k, j)], ACT.Copy
                                   ).then_inc(s_ph, 1)

                for j in range(0, nt, 2):
                    if j == 0:
                        for jj in range(min(2, nt)):
                            copy_transposed(jj)
                    for jj in range(j, min(j + 2, nt)):
                        copy_neighbour(jj)
                    for jj in range(j + 2, min(j + 4, nt)):
                        copy_transposed(jj)
                    for jj in range(j, min(j + 2, nt)):
                        high_part(jj)

            chunks(act, layer3)

        @block.vector
        def _(dve):
            done = [0]

            def link(ins):
                done[0] += 1
                ins.then_inc(s_v, 1)
                dve.wait_ge(s_v, done[0])

            dve.memset(ints[:, 0, (GK - 1) * GE:], 0)
            dve.memset(ints[:, 1, (GK - 1) * GE:], NOWHERE)
            dve.memset(lastd, 0)
            dve.memset(mhalf, -0.5)
            dve.memset(zero16[:, :], 0.0)
            dve.memset(one16[:, :], 1.0)
            dve.memset(zero32[:, :], 0.0)
            link(dve.memset(steptab[:, :, NS:NSP], 0.0))
            dve.sem_inc(s_dc, 1)

            dve.wait_ge(s_edges, 16 * 6)
            dve.wait_ge(s_prev, 16 * GK)
            dve.wait_ge(s_pc, 1)
            srcf, dstf = flts[:, 0, :], flts[:, 1, :]
            lo16, key16, wd16 = (q16[:, q, :, :].rearrange("p k e -> p (k e)") for q in (1, 0, 2))
            dve.tensor_copy(gprev, lastd)
            link(dve.tensor_copy(flts, ints))
            scaled = ((hi, srcf, TR), (wd, dstf, WIN), (gprev, gprev, WIN))
            for a, b, size in scaled:
                last = dve.tensor_scalar(a, b, (size - 1) / 2, 1.0 / size, ALU.subtract, ALU.mult)
            link(last)
            for op in (ALU.add, ALU.subtract):
                for a, b, size in scaled:
                    last = dve.tensor_scalar(a, a, ROUND, None, op)
                link(last)
            dve.scalar_tensor_tensor(lo16, hi, -float(TR), srcf, ALU.mult, ALU.add)
            dve.tensor_copy(wd16, wd)
            dve.tensor_tensor(gend, wd.rearrange("p (k e) -> p k e", e=GE)[:, :, GE - 1], gidx, ALU.add)
            dve.scalar_tensor_tensor(gprev, gprev, -1.0, gidx, ALU.add, ALU.add)
            dve.tensor_copy(gcol16, gidx.unsqueeze(2).broadcast_to([128, GK, 128]))
            link(dve.scalar_tensor_tensor(dstf, wd, -float(WIN), dstf, ALU.mult, ALU.add))
            link(dve.scalar_tensor_tensor(key16, hi, float(WIN), dstf, ALU.mult, ALU.add))
            for k in range(GK):
                link(dve.tensor_scalar(grouphot[:, k, :], iota_s, gprev[:, k:k + 1], None, ALU.is_gt))
                link(dve.scalar_tensor_tensor(grouphot[:, k, :], iota_s, gend[:, k:k + 1], grouphot[:, k, :],
                                              ALU.is_le, ALU.mult))
            dve.tensor_scalar(minus16[:, :], ident[:, 0:TR], -1.0, None, ALU.mult)
            dve.tensor_copy(ident16[:, :], ident[:, 0:TR]).then_inc(s_diag, 1)
            dve.wait_ge(s_sel, 1)

            def halves(a):
                return a.rearrange("p (b s) -> p b s", b=2)

            link(dve.scalar_tensor_tensor(halves(bstep), P[:, 6:8, 0:SH], -1.0, halves(iota_s), ALU.mult, ALU.add))
            dve.tensor_scalar(steps_off[0:1, :], bstep[0:1, :], float(WIN), float(WIN * (NW - 1)),
                              ALU.mult, ALU.min)
            link(dve.tensor_tensor(halves(tmpk), halves(bstep), P[:, 4:6, 0:SH], ALU.is_equal))
            dve.scalar_tensor_tensor(halves(steptab[:, 0, 0:NS]), P[:, 0:2, 0:SH], 1.0, halves(tmpk),
                                     ALU.add, ALU.mult)
            link(dve.tensor_copy(halves(steptab[:, 1, 0:NS]), P[:, 2:4, 0:SH]))
            dve.sem_inc(s_tab, 1)

            def keyhots(s, slot):
                dve.tensor_scalar(keyhot[:, slot, :], iota_key, steptab[:, 0, bass.ds(s, 1)], None,
                                  ALU.is_equal).then_inc(s_key, 1)

            for s in range(AHEAD):
                keyhots(s, s)
            dve.wait_ge(s_zero, 2)
            step = AC + TR
            d = AT[0:TR, 0:(NT - 1) * step].rearrange("p (t c) -> p t c", c=step)[:, :, 0:TR]
            dve.tensor_copy(d, ident16[0:TR, :].unsqueeze(1).broadcast_to([TR, NT - 1, TR]))
            d = AT[0:TR, (NT - 1) * step:(NT - 1) * step + TR]
            link(dve.tensor_copy(d, ident16[0:TR, :]))
            dve.sem_inc(s_add, 1)
            with dve.Fori(0, NS // UNROLL) as turn:
                s = turn * UNROLL
                _, place0 = nc.values_load_multi_w_load_instructions(
                    steps_off[0:1, bass.ds(s, UNROLL)], engines=[mybir.EngineType.DVE],
                    min_val=0, max_val=WIN * (NW - 1),
                    skip_runtime_bounds_check_because="windows are numbered 0 to NW - 1")
                for u in range(UNROLL):
                    keyhots(s + u + AHEAD, (u + AHEAD) % RING)
                    dve.wait_ge(s_cp, s + u + 1)
                    dve.wait_ge(s_add, s + u + 1)
                    place = ATt[:, :, bass.ds(place0[u], WIN)]
                    dve.tensor_tensor(place, place, counted[:, u % RING, :]
                                      .rearrange("p (t c) -> p t c", c=WIN), ALU.add).then_inc(s_add, 1)

            dve.memset(cols, 0.0)
            dve.wait_ge(s_wts, 16 * 6)
            link(dve.tensor_copy(BR[:, :, :], B12[:, :, :]))
            link(dve.tensor_tensor(BR[64:128, :, :], B12[64:128, :, :], BR[64:128, :, :], ALU.subtract))
            dve.tensor_reduce(blocksel[:, :], ident.rearrange("p (q t) -> p t q", q=4)[:, 0:NT, :],
                              axis=mybir.AxisListType.X, op=ALU.add)
            dve.wait_ge(s_dcol, 1)
            link(dve.tensor_scalar(deg, P[0:TR, 4, 0:NT], 1.0, None, ALU.add))
            dve.sem_inc(s_degc, 1)
            link(dve.reciprocal(rdeg, deg))
            link(dve.tensor_scalar(rneigh, deg, -1.0, 1.0, ALU.add, ALU.max))
            link(dve.reciprocal(rneigh, rneigh))
            dve.sem_inc(s_rd, 1)

            for t in range(NT):
                dve.wait_ge(s_pow, 1 if t < FIRST else 2)
                dve.wait_ge(s_xh, t + 1)
                dve.scalar_tensor_tensor(Xt[0:TR, t, 1, :], St[0:TR, t % 8, :], dinv[:, t:t + 1],
                                         Xt[0:TR, t, 0, :], ALU.mult, ALU.subtract).then_inc(s_x1, 1)

            link(dve.tensor_tensor(sdeg, deg, dinv, ALU.mult))
            link(dve.tensor_copy(sd16[:, 0, :], sdeg))
            link(dve.tensor_tensor(sd16[:, 1, :], sdeg, sd16[:, 0, :], ALU.subtract))
            colsq = cols.rearrange("p (a q t) -> p a q t", a=2, q=2)
            for a in range(2):
                last = dve.tensor_copy(colsq[:, a, :, 0:NT], sd16)
            link(last)
            dve.sem_inc(s_sdc, 1)
            dve.wait_ge(s_sdt, 1)
            link(dve.tensor_copy(sdT16[:, :], P[:, 4, 0:TR]))

            def diagonals(i):
                t0, nt = chunk(i)
                for j in range(nt):
                    last = dve.tensor_scalar(DGt[:, j, :], sdT16[:, :], blocksel[:, bass.ds(t0 + j, 1)],
                                             None, ALU.mult)
                last.then_inc(s_dg, 1)

            def low_parts(i, l):
                t0, nt = chunk(i)
                for j in range(nt):
                    if j % 2 == 0:
                        dve.wait_ge(s_ph, NT * l + first_of(i) + min(j + 2, nt))
                    dve.scalar_tensor_tensor(parts_out[0:TR, j, 1, :],
                                             P[0:TR, 6 + j // 2, (j % 2) * D:(j % 2 + 1) * D],
                                             rdeg[:, bass.ds(t0 + j, 1)], parts_out[0:TR, j, 0, :],
                                             ALU.mult, ALU.subtract).then_inc(s_pl, 1)

            def layer1(i, k):
                nt = chunk(i)[1]
                if k:
                    dve.wait_ge(s_w1, i)
                diagonals(i)
                dve.wait_ge(s_w1, i + 1)
                if k:
                    dve.wait_ge(s_wx, i)
                dve.tensor_scalar(hT[:, :, 0:nt * TR], P[:, 4:6, 0:nt * TR], 0.0, None, ALU.max).then_inc(s_h, 1)
                low_parts(i, 0)

            chunks(dve, layer1)

            def layer2(i, k):
                nt = chunk(i)[1]
                if k:
                    dve.wait_ge(s_used, NC * (NC + i))
                diagonals(i)
                dve.wait_ge(s_used, NC * (NC + i + 1))
                dve.wait_ge(s_wx, NC + i)
                b = 2 * ((NC + k) % 2)
                dve.tensor_scalar(hT[:, :, 0:nt * TR], P[:, b:b + 2, 0:nt * TR], 0.0, None, ALU.max
                                  ).then_inc(s_h, 1)
                low_parts(i, 1)

            chunks(dve, layer2)

            def normalise(i, k, li, bank, scale, count):
                t0, nt = chunk(i)
                base = done[0]
                for j in range(nt):
                    last = dve.scalar_tensor_tensor(ring_tile(k, j),
                                                    P[0:TR, bank + j // 2, (j % 2) * D:(j % 2 + 1) * D],
                                                    scale[:, bass.ds(t0 + j, 1)], ring_tile(k, j),
                                                    ALU.mult, ALU.add)
                last.then_inc(s_aev, 1)
                dve.wait_ge(s_aev, NC + li + 1)
                for j in range(nt):
                    last = dve.bn_stats(stats[0:TR, j, :], ring_tile(k, j))
                last.then_inc(s_v, 1)
                dve.wait_ge(s_v, base + li + 1)
                dve.nop(nofuse=True)
                for j in range(nt):
                    last = dve.bn_aggr(mv[0:TR, j, :], stats[0:TR, j, :])
                last.then_inc(s_mv, 1)
                dve.wait_ge(s_rs, li + 1)
                dve.wait_ge(s_mv, li + 1)
                for j in range(nt):
                    dve.tensor_scalar(ring_tile(k, j), ring_tile(k, j), mv[0:TR, j, 0:1], rstd[0:TR, j:j + 1],
                                      ALU.subtract, ALU.mult).then_inc(s_ln, 1)

            rounds = TOPK // 8

            def layer3(i, k):
                t0, nt = chunk(i)
                dve.wait_ge(s_used, NC * (2 * NC + i + 1))
                dve.wait_ge(s_xb, i + 1)
                normalise(i, k, i, 2 * ((2 * NC + k) % 2), dinv, 0)
                def base(j):
                    dve.wait_ge(s_hh, first_of(i) + j + 1)
                    dve.tensor_tensor(ring_tile(k, j), ring_tile(k, j), P[0:TR, 6 + slot2(k, j), 0:D], ALU.add
                                      ).then_inc(s_bs, 1)

                for j0 in range(0, nt, 2):
                    pair = range(j0, min(j0 + 2, nt))
                    for j in pair:
                        base(j)
                    n = 2 * rounds * (first_of(i) + j0)
                    m = len(pair)
                    dve.wait_ge(s_hn, first_of(i) + pair[-1] + 1)
                    dve.nop(nofuse=True)
                    for r in range(rounds):
                        for j in pair:
                            v = j - j0
                            row = neigh_left[v] if r else neigh_row[slot2(k, j)]
                            if r:
                                dve.wait_ge(s_topk, n + 2 * m * r - m + v + 1)
                                dve.nop(nofuse=True)
                            dve.max(top8[0:TR, v, r, :], row).then_inc(s_topk, 1)
                        for j in pair:
                            v = j - j0
                            row = neigh_left[v] if r else neigh_row[slot2(k, j)]
                            dve.wait_ge(s_topk, n + 2 * m * r + v + 1)
                            dve.nop(nofuse=True)
                            dve.match_replace(neigh_left[v], top8[0:TR, v, r, :], row, GONE).then_inc(s_topk, 1)
                    for j in pair:
                        dve.wait_ge(s_topk, n + 2 * m * rounds - m + (j - j0) + 1)
                        dve.scalar_tensor_tensor(neigh_row[slot2(k, j)], neigh_left[j - j0], GONE,
                                                 neigh_row[slot2(k, j)], ALU.is_le, ALU.mult).then_inc(s_sp, 1)

            chunks(dve, layer3)

            def layer4(i, k):
                dve.wait_ge(s_used, NC * (3 * NC + i + 1))
                dve.wait_ge(s_xr[k % 2], 16 * (4 - k % 2) + 8 * (i + 2 - k % 2))
                normalise(i, k, NC + i, 2 * ((3 * NC + k) % 2), rneigh, NT)

            chunks(dve, layer4)

        @block.tensor
        def _(pe):
            pe.wait_ge(s_diag, 1)
            for q in range(4):
                for b in range(2):
                    for k in range(GK):
                        n = GL if k == GK - 1 else 128
                        lhs = gcol16[0:n, k, :] if q == 3 else q16[0:n, q, k, :]
                        last = pe.matmul(P[:, 2 * q + b, 0:SH], lhs, grouphot[0:n, k, b * SH:(b + 1) * SH],
                                         start=k == 0, stop=k == GK - 1)
            last.then_inc(s_sel, 1)

            pe.wait_ge(s_tab, 1)
            pe.sem_inc(s_cnt, LORING)
            with pe.Fori(0, NS // UNROLL) as turn:
                s = turn * UNROLL
                for u in range(UNROLL):
                    pe.wait_ge(s_key, s + u + 1)
                    pe.wait_ge(s_lo, s + u + 2)
                    pe.matmul(P[:, u % RING, 0:KEYS], lohot[:, u % LORING, :], keyhot[:, u % RING, :],
                              start=True, stop=True).then_inc(s_cnt, 1)

            pe.wait_ge(s_sums, 16 * 3)
            for t in range(NT):
                last = pe.matmul(P[0:TR, 4, t:t + 1], sums[:, t * TR:(t + 1) * TR], one16[0:3 * NT, 0:1],
                                 start=True, stop=True)
            last.then_inc(s_dcol, 1)

            def agg_group(k, l, t0, nt, tile, n, first, final):
                if first and l >= 2:
                    for j in range(0, nt, 2):
                        w = min(2, nt - j) * D
                        pe.matmul(P[0:TR, 2 * (k % 2) + j // 2, 0:w], zero16[0:TR, :], AT[0:TR, 0:w],
                                  start=True, stop=False)
                for u in range(n):
                    t = tile + u
                    if l < 2:
                        rhs = AT[0:TR, bass.ds(t * AC + t0 * TR, nt * TR)]
                        for h in range(2):
                            for a in range(2):
                                lhs = X[0:TR, bass.ds(t * 2 * D + a * D + h * 128, 128)]
                                last = pe.matmul(P[:, 2 * (k % 2) + h, 0:nt * TR], lhs, rhs,
                                                 start=first and u == 0 and a == 0,
                                                 stop=final and u == n - 1 and a == 1)
                    else:
                        for j in range(nt):
                            lhs = AT[0:TR, bass.ds(t * AC + (t0 + j) * TR, TR)]
                            for a in range(2):
                                rhs = X[0:TR, bass.ds(t * 2 * D + a * D, D)]
                                last = pe.matmul(P[0:TR, 2 * (k % 2) + j // 2, (j % 2) * D:(j % 2 + 1) * D],
                                                 lhs, rhs, start=False,
                                                 stop=final and u == n - 1 and a == 1
                                                 and (j % 2 == 1 or j == nt - 1))
                return last

            def aggregate(i, k, l, between):
                t0, nt = chunk(i)
                kk = NC * l + k
                for q in range(NC):
                    if k == 0 and l == 0:
                        pe.wait_ge(s_x1, 4 * q + 1)
                    elif k == 0:
                        pe.wait_ge(s_re[q], 16 * l)
                    if l == 3 and q == NC - 1:
                        for j in range(nt):
                            for a in range(2):
                                pe.matmul(P[0:TR, 2 * (kk % 2) + j // 2, (j % 2) * D:(j % 2 + 1) * D],
                                          minus16[0:TR, :], X[0:TR, bass.ds((t0 + j) * 2 * D + a * D, D)],
                                          start=False, stop=False)
                    last = agg_group(kk, l, t0, nt, 0 if q == 0 else 4 * q - 3, 1 if q == 0 else CT,
                                     q == 0, q == NC - 1)
                    last.then_inc(s_used, 1)
                    between(q)

            def diag_bias(bank, l, nt):
                for h in range(2):
                    pe.matmul(P[:, bank + h, 0:nt * TR], BR[:, l, 128 * h:128 * h + 128], DG16[:, 0:nt * TR],
                              start=False, stop=False)

            def apply_w1(i):
                t0, nt = chunk(i)
                pe.wait_ge(s_aev, i + 1)
                pe.wait_ge(s_dg, i + 1)
                for kt in range(2):
                    for h in range(2):
                        last = pe.matmul(P[:, 4 + h, 0:nt * TR], W[:, kt, 128 * h:128 * h + 128],
                                         aggT[:, kt, 0:nt * TR], start=kt == 0, stop=kt == 1)
                    if kt == 0:
                        diag_bias(4, 0, nt)
                last.then_inc(s_w1, 1)

            def next_operand(i, l):
                nt = chunk(i)[1]
                pe.wait_ge(s_h, NC * l + i + 1)
                if not (isinstance(i, int) and i == 0 and l == 0):
                    pe.wait_ge(s_pl, NT * l + first_of(i))
                for j in range(nt):
                    for kt in range(2):
                        w = W[:, kt, D:2 * D] if l == 0 else W3[:, kt, :]
                        last = pe.matmul(P[0:TR, 6 + j // 2, (j % 2) * D:(j % 2 + 1) * D],
                                         hT[:, kt, j * TR:(j + 1) * TR], w, start=kt == 0, stop=kt == 1)
                last.then_inc(s_wx, 1)

            pe.wait_ge(s_wts, 16 * 6)

            def before(i, k):
                return (i - 1, k - 1) if k else (NC - 1, NC - 1)

            def layer1(i, k):
                def between(q):
                    if k == 0 and q == NC - 1:
                        pe.wait_ge(s_sdc, 1)
                        pe.transpose(P[:, 4, 0:TR], cols, ident[0:TR, 0:TR]).then_inc(s_sdt, 1)
                    if k and q == 2:
                        apply_w1(i - 1)
                    if k and q == 5:
                        next_operand(i - 1, 0)
                if k >= 2:
                    pe.wait_ge(s_aev, i - 1)
                aggregate(i, k, 0, between)

            def layer2(i, k):
                def between(q):
                    if k == 0 and q == 0:
                        apply_w1(NC - 1)
                    if q == 3:
                        next_operand(before(i, k)[0], 1 if k else 0)
                    if q == 5:
                        pe.wait_ge(s_dg, NC + i + 1)
                        diag_bias(2 * ((NC + k) % 2), 1, chunk(i)[1])
                pe.wait_ge(*((s_aev, 6 + i) if k < 2 else (s_h, NC + i - 1)))
                aggregate(i, k, 1, between)

            def transpose_x1(i, k, j):
                o = first_of(i) + j
                pe.wait_ge(s_ln, o + 1)
                if k or j >= 2:
                    pe.wait_ge(s_tc, o - 1)
                for h in range(2):
                    last = pe.transpose(P[:, 4 + slot2(k, j), h * TR:(h + 1) * TR],
                                        ring_tile(k, j)[:, 128 * h:128 * h + 128], ident[0:TR, 0:TR])
                last.then_inc(s_tr, 1)

            def self_and_neighbour(i, k, j):
                o = first_of(i) + j
                pe.wait_ge(s_tc, o + 1)
                if k or j >= 2:
                    pe.wait_ge(s_bs, o - 1)
                    pe.wait_ge(s_hn, o - 1)
                for h in range(2):
                    last = pe.matmul(P[0:TR, 6 + slot2(k, j), :], x1T[slot2(k, j)][:, h, :], W[:, h, :],
                                     start=h == 0, stop=h == 1)
                last.then_inc(s_hh, 1)

            def tile_work(i, k, q):
                nt = chunk(i)[1]
                for j in range(nt):
                    if q == (2 if j < 2 else 3):
                        if j == 2:
                            self_and_neighbour(i, k, 0)
                            self_and_neighbour(i, k, 1)
                        transpose_x1(i, k, j)
                    if q == 2 + j and j >= 2 or nt == 1 and q == 3:
                        self_and_neighbour(i, k, j)

            def layer3(i, k):
                def between(q):
                    if k == 0 and q == 3:
                        next_operand(NC - 1, 1)
                    if k:
                        tile_work(i - 1, k - 1, q)
                    if k == 0 and q == 3:
                        pe.wait_ge(s_wn, 32)
                pe.wait_ge(*((s_h, 2 * NC - 1 + i) if k < 2 else (s_aev, NC + i - 1)))
                aggregate(i, k, 2, between)

            def layer4(i, k):
                def between(q):
                    if k == 0:
                        tile_work(NC - 1, 4, q + 1)
                pe.wait_ge(s_aev, 2 * NC + i - 1)
                aggregate(i, k, 3, between)

            chunks(pe, layer1)
            chunks(pe, layer2)
            chunks(pe, layer3)
            chunks(pe, layer4)


def kernel(x, src, dst, L0_gnn_W1, L0_gnn_b1, L0_gnn_W2, L0_gnn_b2, L0_gnn_W3, L0_gnn_b3, L1_gnn_W_self,
           L1_gnn_W_neigh):
    import concourse.bacc as bacc
    from concourse.bass_utils import run_bass_kernel_spmd as run

    nc = bacc.Bacc("TRN2", target_bir_lowering=False, num_devices=1)
    arrays, args = {}, []
    given = [("x", x), ("src", src), ("dst", dst), ("w1", L0_gnn_W1), ("b1", L0_gnn_b1), ("w2", L0_gnn_W2),
             ("b2", L0_gnn_b2), ("w3", L0_gnn_W3), ("b3", L0_gnn_b3), ("wself", L1_gnn_W_self),
             ("wneigh", L1_gnn_W_neigh)]
    for name, a in given:
        a = np.ascontiguousarray(a)
        arrays[f"in_{name}"] = a
        args.append(nc.dram_tensor(f"in_{name}", a.shape, mybir.dt.from_np(a.dtype), kind="ExternalInput").ap())
    args.append(nc.dram_tensor("out", (N, D), F32, kind="ExternalOutput").ap())
    gnn(nc, *args)
    r = run(nc, [arrays], core_ids=[0])
    return r.results[0]["out"]
```

```python
import numpy as np
import concourse.bass as bass
from concourse import mybir
from concourse.alu_op_type import AluOpType as ALU

F32 = mybir.dt.float32
F16 = mybir.dt.float16
I32 = mybir.dt.int32
ACT = mybir.ActivationFunctionType

N = 3125
E = 50000
D = 256
TR = 125
NT = N // TR
HB = D // 128

WIN = 16
NW = -(-N // WIN)
AC = NW * WIN
GE = 128
NG = -(-E // GE)
GK = -(-NG // 128)
GL = NG - 128 * (GK - 1)
ELAST = E - GE * (NG - 1)
UNROLL = 28
NS = -(-(NW + NG - 1) // UNROLL) * UNROLL
DVE_LO = (12,)
PER_TURN = UNROLL - len(DVE_LO)
AHEAD = 6
RING = AHEAD + 1
ATONCE = 2
BANKS = 4
NSP = NS + RING
LORING = UNROLL // 2
NOWHERE = 32000
ROUND = 1.5 * 2 ** 23

CT = 4
CW = CT * TR
NC = 1 + (NT - 1) // CT
XP = NT - NS // UNROLL
FIRST = 5
TOPK = 32
PRODUCTS = ((0, 0), (0, 1), (1, 0))
WS = 64.0
GONE = -3.0e38
WORDS = NT * AC // 2
ZP, ZD = WORDS * 2 // 5, WORDS * 3 // 20
ZA = [ZP + ZD] + [ZP + ZD + (WORDS - ZP - ZD) * (5 + i) // (9 + XP) for i in range(XP + 1)] + [WORDS]


def chunk(i):
    if isinstance(i, int) and i < 2:
        return (1, CT) if i == 0 else (0, 1)
    return CT * i - (CT - 1), CT


def first_of(i):
    if isinstance(i, int) and i < 2:
        return CT * i
    return CT * i - (CT - 1)


def pairs(nt):
    return [(j, min(j + 2, nt)) for j in range(0, nt, 2)]


def pairs_before(i):
    if isinstance(i, int) and i < 2:
        return 2 * i
    return 2 * i - 1


PAIRS = pairs_before(NC)


def gnn(nc, x, src, dst, w1, b1, w2, b2, w3, b3, wself, wneigh, out):
    def sb(name, shape, dt):
        return nc.alloc_sbuf_tensor(name, shape, dt).ap()

    def sem(name):
        return nc.alloc_semaphore(name)

    xparts_dram = [nc.dram_tensor(f"xparts{l}", (NT, TR, 2 * D), F16, kind="Internal").ap() for l in range(3)]
    xw_dram = nc.dram_tensor("xw", (NT, TR, D), F32, kind="Internal").ap()
    base_dram = nc.dram_tensor("base", (NT, TR, D), F32, kind="Internal").ap()

    AT = sb("AT", [128, NT * AC], F16)
    XS0 = 2 * 14 * D
    SX = sb("SX", [128, XS0 + NT * 2 * D], F16)
    S = SX[:, 0:XS0].bitcast(F32)
    X = SX[:, XS0:]
    W = sb("W", [128, HB, 2 * D], F32)
    W3 = sb("W3", [128, HB, D], F32)
    DG = sb("DG", [128, CT * TR], F32)
    B12 = sb("B12", [128, 2, D], F32)
    B3 = sb("B3", [128, D], F32)
    ident = sb("ident", [128, 128], F32)
    ident16 = sb("ident16", [128, TR], F16)
    minus16 = sb("minus16", [128, TR], F16)
    one16 = sb("one16", [128, 32], F16)
    zero32 = sb("zero32", [128, 1], F32)
    tabs = sb("tabs", [128, 8, NT], F32)
    deg, dinv, sdeg, rdeg, rneigh = (tabs[0:TR, i, :] for i in range(5))
    mhalf = tabs[0:TR, 5, :]
    steps_off = sb("steps_off", [1, NS], I32)
    stats = sb("stats", [128, CT, 6], F32)
    mv = sb("mv", [128, CT, 2], F32)
    rstd = sb("rstd", [128, CT], F32)
    ATt = AT.rearrange("p (t c) -> p t c", t=NT)
    Xt = X.rearrange("p (t a d) -> p t a d", t=NT, a=2)
    St = S.rearrange("p (k d) -> p k d", d=D)
    cols = St[0:TR, 12, 0:128]
    sdT16 = St[:, 12, 128:192].bitcast(F16)[:, 0:TR]
    sd16 = St[0:TR, 12, 192:192 + NT].bitcast(F16).rearrange("p (a t) -> p a t", a=2)
    blocksel = St[:, 12, 224:224 + NT]
    BR = St[:, 13, :].bitcast(F16).rearrange("p (l d) -> p l d", l=2)
    top8 = B12[:, 0, 0:2 * TOPK].rearrange("p (v r e) -> p v r e", v=2, e=8)
    DG16 = DG[:, 0:CT * TR // 2].bitcast(F16)
    DGt = DG16.rearrange("p (j n) -> p j n", j=CT)

    KEYS = NT * WIN
    o = 0
    keyhot = X[:, o:o + RING * KEYS].rearrange("p (r n) -> p r n", r=RING)
    o += RING * KEYS
    GX = GK * GE
    hi = X[:, o:o + 2 * GX].bitcast(F32)
    o += 2 * GX
    wd = X[:, o:o + 2 * GX].bitcast(F32)
    ended = X[:, 0:GK * NS].rearrange("p (k s) -> p k s", k=GK)
    assert GK * NS <= RING * KEYS
    lohot = X[:, o - 2 * GX:o - 2 * GX + LORING * 128].rearrange("p (r n) -> p r n", r=LORING)
    assert LORING * 128 <= 4 * GX
    o += 2 * GX
    counted = X[:, o:o + RING * KEYS].rearrange("p (r n) -> p r n", r=RING)
    assert RING * KEYS <= 4 * GX + GK * NS
    q16 = X[:, o:o + 3 * GX].rearrange("p (q k e) -> p q k e", q=3, k=GK)
    o += 3 * GX
    gcol16 = X[:, o:o + GX].rearrange("p (k m) -> p k m", k=GK)
    o += GX
    grouphot = X[:, o:o + GK * NS].rearrange("p (k s) -> p k s", k=GK)
    o += GK * NS
    iota_key = X[:, o:o + KEYS]
    o += KEYS
    iota_lo = X[:, o:o + 126]
    o += 126
    xt0 = NT * 2 * D - 3 * 2 * D
    x_tile = X[0:TR, xt0:].bitcast(F32).rearrange("p (r d) -> p r d", r=3)
    assert o <= xt0, o
    sums = X[0:3 * NT, NT * 2 * D - N:]
    o = 0
    steptab = S[:, o:o + 2 * NSP].rearrange("p (q s) -> p q s", q=2)
    o += 2 * NSP
    iota_s = S[:, o:o + NS // 2].bitcast(F16)
    o += NS // 2
    assert NS <= 2048
    turn_lo = S[:, o:o + UNROLL]
    o += UNROLL
    gend = S[:, o:o + GK]
    o += GK
    gprev = S[:, o:o + GK]
    o += GK
    gidx = S[:, o:o + GK]
    o += GK
    lastd = S[:, o:o + GK].bitcast(I32)
    o += GK
    bstep = S[:, o:o + NS]
    tmpk = S[:, o + NS:o + 2 * NS]
    ints = S[:, o:o + 2 * GX].bitcast(I32).rearrange("p (q e) -> p q e", q=2)
    flts = S[:, o:o + 2 * GX].rearrange("p (q e) -> p q e", q=2)
    o += max(2 * NS, 2 * GX)
    assert o <= 12 * D, o
    xT = DG.rearrange("p (r h n) -> p r h n", r=2, h=2)
    xw_tile = St[0:TR, 12:14, :]
    SH = NS // 2

    P = nc.alloc_psum_tensor("P", [128, 8, 512], F32).ap()

    s_edges = sem("edges_loaded")
    s_prev = sem("previous_dst_loaded")
    s_w1 = sem("w1_loaded")
    s_wts = sem("weights_loaded")
    s_pc = sem("pool_constants_ready")
    s_dc = sem("dve_constants_ready")
    s_v = sem("dve_step_done")
    s_p = sem("pool_step_done")
    s_zero = sem("at_zeroed")
    s_sel = sem("edges_selected")
    s_places = sem("source_places_ready")
    s_tab = sem("step_tables_ready")
    s_key = sem("keyhot_ready")
    s_lo = sem("lohot_ready")
    s_dlo = sem("dve_lohot_ready")
    s_turn = sem("turn_columns_copied")
    s_cnt = sem("window_counted")
    s_cp = sem("counted_copied")
    s_add = sem("counted_added")
    s_diag = sem("group_one_hots_and_identities_ready")
    s_loops = sem("self_loops_set")
    s_sums = sem("source_tile_sums_moved")
    s_dcol = sem("degree_columns_ready")
    s_degc = sem("degrees_copied")
    s_sdc = sem("sqrt_degree_columns_ready")
    s_sdt = sem("sqrt_degrees_transposed")
    s_pow = sem("degree_powers_ready")
    s_rd = sem("degree_tables_ready")
    s_ident = sem("identity_ready")
    s_xin = [sem(f"x_tile_loaded{i}") for i in range(3)]
    s_xt = sem("x_tile_transposed")
    s_xtc = sem("x_transpose_copied")
    s_xm = sem("x_tile_multiplied")
    s_xmc = sem("x_product_copied")
    s_xws = [sem(f"x_product_stored{i}") for i in range(2)]
    s_xl = [sem(f"x_product_loaded{i}") for i in range(2)]
    s_xh = sem("first_operand_high_ready")
    s_x1 = sem("first_operand_ready")
    s_aev = sem("chunk_evacuated")
    s_dg = sem("diagonals_ready")
    s_h = sem("hidden_ready")
    s_wx = sem("next_operand_multiplied")
    s_ph = sem("high_parts_ready")
    s_pl = sem("low_parts_ready")
    s_st = sem("parts_stored")
    s_st3 = [sem(f"last_parts_stored{i}") for i in range(2)]
    s_used = sem("operand_tiles_used")
    s_re = [sem(f"operand_reloaded{i}") for i in range(NC - 1)]
    s_xr = [sem(f"residual_loaded{i}") for i in range(2)]
    s_xb = sem("residual_and_bias_ready")
    s_mv = sem("mean_and_variance_ready")
    s_rs = sem("rstd_ready")
    s_ln = sem("normalised")
    s_tr = sem("x1_transposed")
    s_tc = sem("x1_transpose_high_copied")
    s_tl = sem("x1_transpose_low_copied")
    s_hhi = sem("hidden_high_ready")
    s_w4 = sem("self_and_neighbour_weights_split")
    s_hh = sem("self_and_neighbour_ready")
    s_hn = sem("neighbour_copied")
    s_bs = sem("base_ready")
    s_bst = [sem(f"base_stored{i}") for i in range(2)]
    s_sp = sem("sparse_ready")
    s_wn = sem("neighbour_weights_loaded")
    s_topk = sem("topk_step_done")
    s_out = [sem(f"out_stored{i}") for i in range(2)]

    sum_rows = [ATt[TR + c:TR + c + 1, :, 0:N] for c in range(3)]

    def parts_rows(l, t0, nt):
        return xparts_dram[l][bass.ds(t0, nt), :, :].rearrange("t p e -> p t e")

    def tile_rows(a, t0, nt):
        return a[bass.ds(t0, nt), :, :].rearrange("t p d -> p t d")

    x_t = x.rearrange("(t p) d -> t p d", p=TR)
    out_t = out.rearrange("(t p) d -> t p d", p=TR)
    parts_out = S[:, 8 * D:12 * D].bitcast(F16).rearrange("p (j a d) -> p j a d", j=CT, a=2)

    def part_place(i, k, j, a):
        out = 16 * D + (2 * j + a) * D
        there = XS0 + ((NT - CT + j) * 2 + a) * D
        if k == 4:
            return SX[0:TR, bass.ds((i - 4) * ((there - out) // 2) + out, D)]
        return SX[0:TR, out:out + D]

    hT = (St[:, 4:8, :].rearrange("p k d -> p (k d)")[:, 0:2 * CW].bitcast(F16)
          .rearrange("p (a h n) -> p a h n", a=2, h=2))
    W2p = B12.rearrange("p a d -> p (a d)").bitcast(F16).rearrange("p (k a d) -> p k a d", k=2, a=2)
    W3p = [W[:, k, D:2 * D].bitcast(F16).rearrange("p (a d) -> p a d", a=2) for k in range(HB)]
    W4raw = St[:, 0:4, :].rearrange("p (k c) d -> p k (c d)", k=2)
    W4p = [[W[:, k, 0:D].bitcast(F16), W3[:, k, :].bitcast(F16)] for k in range(HB)]
    NXG = -(-NT // 4)

    def xslot(t, n):
        return t % n if isinstance(t, int) else 0

    def xbefore(t, n):
        return t - n + 1 if isinstance(t, int) else t

    def chunks(eng, step):
        for i in range(3):
            step(i, i)
        with eng.Fori(0, (NC - 3) // 2) as turn:
            step(2 * turn + 3, 3)
            step(2 * turn + 4, 4)

    def slot2(k, j):
        return (first_of(k) + j) % 2

    def ring_slots(k, nt):
        return St[0:TR, 4 * (k % 2):4 * (k % 2) + nt, :]

    def ring_tile(k, j):
        return St[0:TR, 4 * (k % 2) + j, :]

    last_parts = [St[0:TR, 8 + r, :].bitcast(F16).rearrange("p (a d) -> p a d", a=2) for r in range(2)]

    def last_part(i, k, j, a):
        out = 16 * D + (2 * slot2(k, j) + a) * D
        there = XS0 + ((NT - CT + j) * 2 + a) * D
        if k == 4:
            return SX[0:TR, bass.ds((i - 4) * ((there - out) // 2) + out, D)]
        return SX[0:TR, out:out + D]

    neigh_row = [St[0:TR, 10, :], St[0:TR, 13, :]]
    neigh_left = [St[0:TR, 11, :], St[0:TR, 12, :]]
    x1T = DG.bitcast(F16).rearrange("p (r a h n) -> p r a h n", r=2, a=2, h=2)

    with nc.Block() as block:

        @block.sync
        def _(sp):
            sp.wait_ge(s_dc, 1)
            full = 128 * (GK - 1)
            for q, a in ((0, src), (1, dst)):
                sp.dma_start(ints[:, q, 0:(GK - 1) * GE].rearrange("p (k e) -> p k e", e=GE),
                             a[0:full * GE].rearrange("(k p e) -> p k e", p=128, e=GE)).then_inc(s_edges, 16)
                sp.dma_start(ints[0:GL - 1, q, (GK - 1) * GE:],
                             a[full * GE:(NG - 1) * GE].rearrange("(g e) -> g e", e=GE)).then_inc(s_edges, 16)
                sp.dma_start(ints[GL - 1:GL, q, (GK - 1) * GE:(GK - 1) * GE + ELAST],
                             a[GE * (NG - 1):E].rearrange("(g e) -> g e", g=1)).then_inc(s_edges, 16)
            last = dst[0:(NG - 1) * GE].rearrange("(g e) -> g e", e=GE)[:, GE - 1:GE]
            sp.dma_start(lastd[1:128, 0:1], last[0:127, :], allow_slow_non_contiguous=True).then_inc(s_prev, 16)
            for k in range(1, GK):
                n = min(128, NG - 128 * k)
                sp.dma_start(lastd[0:n, k:k + 1], last[128 * k - 1:128 * k - 1 + n, :],
                             allow_slow_non_contiguous=True).then_inc(s_prev, 16)
            def load_x(t):
                if not isinstance(t, int) or t >= 3:
                    sp.wait_ge(s_xt, xbefore(t, 3))
                sp.dma_start(x_tile[:, xslot(t, 3):xslot(t, 3) + 1, :], tile_rows(x_t, t, 1)
                             ).then_inc(s_xin[xslot(t, 3)], 16)

            def store_xw(t):
                sp.wait_ge(s_xmc, t + 1)
                sp.dma_start(tile_rows(xw_dram, t, 1), xw_tile[:, xslot(t, 2):xslot(t, 2) + 1, :]
                             ).then_inc(s_xws[xslot(t, 2)], 16)

            load_x(0)
            sp.dma_start(W[:, :, 0:D], w1.rearrange("(h p) d -> p h d", p=128)).then_inc(s_w1, 16)
            load_x(1)
            load_x(2)
            for a, dest in ((w2, W[:, :, D:2 * D]), (w3, W3[:, :, :])):
                sp.dma_start(dest, a.rearrange("(h p) d -> p h d", p=128)).then_inc(s_wts, 16)
            for a, dest in ((b1, B12[:, 0, :]), (b2, B12[:, 1, :]), (b3, B3[:, :])):
                sp.dma_start(dest, a.rearrange("(o d) -> o d", o=1).broadcast_to([128, D])).then_inc(s_wts, 16)
            for t in range(XP):
                if t + 3 < XP:
                    load_x(t + 3)
                store_xw(t)
            with sp.Fori(0, NT - XP) as turn:
                load_x(turn + XP)
                store_xw(turn + XP)
            sp.wait_ge(s_add, NS + 1)
            for c in range(3):
                sp.dma_start(sums[c * NT:(c + 1) * NT, :], sum_rows[c]).then_inc(s_sums, 16)
            sp.wait_ge(s_xws[0], 16 * (NT - XP + (XP + 1) // 2))
            sp.wait_ge(s_xws[1], 16 * (XP // 2))
            for g in range(NXG):
                nt = min(4, NT - 4 * g)
                if g >= 2:
                    sp.wait_ge(s_x1, 4 * (g - 1))
                sp.dma_start(St[0:TR, 4 * (g % 2):4 * (g % 2) + nt, :],
                             tile_rows(xw_dram, 4 * g, nt)).then_inc(s_xl[g % 2], 16)

            sp.wait_ge(s_x1, NT)
            for c, a in ((0, wself), (1, wneigh)):
                sp.dma_start(W4raw[:, :, c * D:(c + 1) * D], a.rearrange("(h p) d -> p h d", p=128)
                             ).then_inc(s_wn, 16)

            def reload(l, groups):
                for q in groups:
                    t0, nt = (0, 1) if q == 0 else (4 * q - 3, CT)
                    i = {0: 1, 1: 0}.get(q, q)
                    if l < 2:
                        sp.wait_ge(s_st, 16 * ((NC - 1) * l + max(i + 1, 2 if q < 2 else 0)))
                    else:
                        done = first_of(i) + nt
                        sp.wait_ge(s_st3[0], 16 * ((done + 1) // 2))
                        sp.wait_ge(s_st3[1], 16 * (done // 2))
                    sp.wait_ge(s_used, NC * NC * l + NC * (NC - 1) + q + 1)
                    sp.dma_start(Xt[0:TR, t0:t0 + nt, :, :].rearrange("p t a d -> p t (a d)"),
                                 parts_rows(l, t0, nt)).then_inc(s_re[q], 16)

            for l in range(2):
                for i in range(NC):
                    t0, nt = chunk(i)
                    if i == NC - 1:
                        reload(l, range(NC - 1))
                    if i < NC - 1:
                        sp.wait_ge(s_ph, NT * l + first_of(i) + nt)
                        sp.wait_ge(s_pl, NT * l + first_of(i) + nt)
                        sp.dma_start(parts_rows(l, t0, nt),
                                     parts_out[0:TR, 0:nt, :, :].rearrange("p j a d -> p j (a d)")
                                     ).then_inc(s_st, 16)

            def load_ring(i, rows):
                t0, nt = chunk(i)
                sp.dma_start(ring_slots(i, nt), tile_rows(rows, t0, nt)).then_inc(s_xr[i % 2], 16)

            sp.wait_ge(s_w4, 1)
            sp.wait_ge(s_wx, 2 * NC)
            load_ring(0, x_t)
            load_ring(1, x_t)
            for i in range(NC):
                t0, nt = chunk(i)
                if i == NC - 1:
                    reload(2, [NC - 2])
                for j in range(nt):
                    if i == NC - 2 and j in (0, 2):
                        reload(2, (0, 1, 2) if j == 0 else range(3, NC - 2))
                    o = first_of(i) + j
                    sp.wait_ge(s_bs, o + 1)
                    sp.dma_start(tile_rows(base_dram, t0 + j, 1), ring_slots(i, nt)[:, j:j + 1, :]
                                 ).then_inc(s_bst[i % 2], 16)
                    if i == NC - 1:
                        continue
                    sp.wait_ge(s_ph, 2 * NT + o + 1)
                    sp.wait_ge(s_pl, 2 * NT + o + 1)
                    sp.dma_start(parts_rows(2, t0 + j, 1), last_parts[o % 2].rearrange("p a d -> p (a d)")
                                 .unsqueeze(1)).then_inc(s_st3[o % 2], 16)
                if i + 2 < NC:
                    sp.wait_ge(s_bst[i % 2], 16 * sum(chunk(c)[1] for c in range(i % 2, i + 1, 2)))
                    load_ring(i + 2, x_t)

            for r in range(2):
                sp.wait_ge(s_bst[r], 16 * sum(chunk(c)[1] for c in range(r, NC, 2)))
            load_ring(0, base_dram)
            load_ring(1, base_dram)
            for i in range(NC):
                t0, nt = chunk(i)
                for a, b in pairs(nt):
                    sp.wait_ge(s_ln, NT + first_of(i) + b)
                    sp.dma_start(tile_rows(out_t, t0 + a, b - a), ring_slots(i, nt)[:, a:b, :]
                                 ).then_inc(s_out[i % 2], 16)
                if i + 2 < NC:
                    sp.wait_ge(s_out[i % 2], 16 * sum(len(pairs(chunk(c)[1])) for c in range(i % 2, i + 1, 2)))
                    load_ring(i + 2, base_dram)
            for r in range(2):
                sp.wait_ge(s_out[r], 16 * sum(len(pairs(chunk(c)[1])) for c in range(r, NC, 2)))

        @block.gpsimd
        def _(pool):
            done = [0]

            def link(ins):
                done[0] += 1
                ins.then_inc(s_p, 1)
                pool.wait_ge(s_p, done[0])

            link(pool.memset(ident[:, :], 0.0))
            link(pool.affine_select(out=ident[:, :], in_=ident[:, :], compare_op=ALU.not_equal, fill=1.0,
                                    base=0, pattern=[[-1, 128]], channel_multiplier=1))
            pool.sem_inc(s_ident, 1)
            link(pool.iota(iota_s, pattern=[[1, NS]], base=0, channel_multiplier=0,
                           allow_small_or_imprecise_dtypes=True))
            link(pool.iota(gidx, pattern=[[128, GK]], base=0, channel_multiplier=1,
                           allow_small_or_imprecise_dtypes=True))
            link(pool.iota(iota_key, pattern=[[1, KEYS]], base=1, channel_multiplier=0,
                           allow_small_or_imprecise_dtypes=True))
            pool.iota(iota_lo, pattern=[[1, 126]], base=0, channel_multiplier=0,
                      allow_small_or_imprecise_dtypes=True).then_inc(s_pc, 1)
            pool.memset(AT[:, 0:2 * ZP].bitcast(F32), 0.0).then_inc(s_zero, 1)

            pool.wait_ge(s_places, 1)
            link(pool.memset(lohot[:, :, TR:128], 0.0))
            for c, (p0, p1) in enumerate(((0, 32), (32, 64), (64, 128))):
                link(pool.memset(lohot[p0:p1, :, TR + c:TR + c + 1], 1.0))
            pool.sem_inc(s_lo, 1)
            with pool.Fori(0, NS // UNROLL) as turn:
                s = turn * UNROLL
                pool.wait_ge(s_lo, turn * PER_TURN + 1)
                pool.nop(nofuse=True)
                pool.tensor_copy(turn_lo, steptab[:, 1, bass.ds(s, UNROLL)]).then_inc(s_turn, 1)
                pool.wait_ge(s_turn, turn + 1)
                for u in range(UNROLL):
                    if u in DVE_LO:
                        continue
                    pool.wait_ge(s_cnt, s + u + 1)
                    pool.nop(nofuse=True)
                    pool.tensor_scalar(lohot[:, u % LORING, 0:TR], iota_lo[:, 0:TR], turn_lo[:, u:u + 1], None,
                                       ALU.is_equal).then_inc(s_lo, 1)

            pool.wait_ge(s_degc, 1)
            for a, b in ((0, FIRST), (FIRST, NT)):
                pool.tensor_tensor(dinv[:, a:b], deg[:, a:b], mhalf[:, a:b], ALU.pow).then_inc(s_pow, 1)

            def finish_rstd(nt, before):
                for h, (a, b) in enumerate(pairs(nt)):
                    pool.wait_ge(s_mv, before + h + 1)
                    pool.nop(nofuse=True)
                    pool.tensor_scalar(rstd[0:TR, a:b], mv[0:TR, a:b, 1], 1e-5, None, ALU.add).then_inc(s_p, 1)
                    pool.wait_ge(s_p, done[0] + before + h + 1)
                    pool.tensor_tensor(rstd[0:TR, a:b], rstd[0:TR, a:b], mhalf[:, a:b], ALU.pow).then_inc(s_rs, 1)

            def add_bias(i):
                nt = chunk(i)[1]
                pool.wait_ge(s_xr[i % 2], 16 * (i // 2 + 1))
                pool.tensor_tensor(ring_slots(i, nt), ring_slots(i, nt),
                                   B3[0:TR, :].unsqueeze(1).broadcast_to([TR, nt, D]), ALU.add).then_inc(s_xb, 1)

            pool.wait_ge(s_wts, 16 * 5)
            add_bias(0)
            for i in range(NC):
                if i != 1:
                    finish_rstd(chunk(i)[1], pairs_before(i))
                if i + 1 < NC:
                    add_bias(i + 1)
                if i == 0:
                    finish_rstd(chunk(1)[1], pairs_before(1))
                for j in range(chunk(i)[1]):
                    o = first_of(i) + j
                    pool.wait_ge(s_ph, 2 * NT + o + 1)
                    hl = Xt[0:TR, chunk(i)[0] + j, :, :] if i == NC - 1 else last_parts[o % 2]
                    pool.tensor_tensor(hl[:, 1, :], neigh_row[o % 2], hl[:, 0, :],
                                       ALU.subtract).then_inc(s_pl, 1)

            def layer4(i, k):
                finish_rstd(chunk(i)[1], PAIRS + pairs_before(i))

            chunks(pool, layer4)

        @block.scalar
        def _(act):
            def copy_transposed_x(t):
                act.wait_ge(s_xt, t + 1)
                if not isinstance(t, int) or t >= 2:
                    act.wait_ge(s_xm, xbefore(t, 2))
                act.activation(xT[:, xslot(t, 2), :, :], P[:, 4 + xslot(t, 2), 0:2 * TR]
                               .rearrange("p (h n) -> p h n", h=2), ACT.Copy).then_inc(s_xtc, 1)

            def copy_product(t):
                act.wait_ge(s_xm, t + 1)
                if not isinstance(t, int):
                    act.wait_ge(s_xws[0], 16 * (t - XP + (XP + 1) // 2))
                elif t >= 2:
                    act.wait_ge(s_xws[t % 2], 16 * (t // 2))
                act.activation(xw_tile[:, xslot(t, 2), :], P[0:TR, 6 + xslot(t, 2), 0:D], ACT.Copy
                               ).then_inc(s_xmc, 1)

            def zero_piece(i):
                a, b = ZA[i:i + 2]
                return act.activation(AT[:, 2 * a:2 * b].bitcast(F32), zero32[:, :].broadcast_to([128, b - a]),
                                      ACT.Copy)

            act.wait_ge(s_dc, 1)
            zero_piece(0)
            for t in range(XP):
                copy_transposed_x(t)
                zero_piece(t + 1)
                copy_product(t)
            zero_piece(XP + 1).then_inc(s_zero, 1)
            act.wait_ge(s_zero, 3)
            act.wait_ge(s_diag, 1)
            step = AC + TR
            d = AT[0:TR, 0:(NT - 1) * step].rearrange("p (t c) -> p t c", c=step)[:, :, 0:TR]
            act.activation(d, ident16[0:TR, :].unsqueeze(1).broadcast_to([TR, NT - 1, TR]), ACT.Copy)
            d = AT[0:TR, (NT - 1) * step:(NT - 1) * step + TR]
            act.activation(d, ident16[0:TR, :], ACT.Copy).then_inc(s_loops, 1)

            act.sem_inc(s_cp, BANKS)
            with act.Fori(0, NS // UNROLL) as turn:
                s = turn * UNROLL
                for u in range(UNROLL):
                    act.wait_ge(s_cnt, LORING + s + u + 1)
                    act.activation(counted[:, u % RING, :], P[:, u % BANKS, 0:KEYS], ACT.Copy).then_inc(s_cp, 1)
                    if u == UNROLL // 4:
                        copy_transposed_x(turn + XP)
                    if u == UNROLL * 3 // 4:
                        copy_product(turn + XP)

            for t in range(NT):
                act.wait_ge(s_pow, 1 if t < FIRST else 2)
                act.wait_ge(s_xl[t // 4 % 2], 16 * (t // 8 + 1))
                act.activation(Xt[0:TR, t, 0, :], St[0:TR, t % 8, :], ACT.Copy,
                               scale=dinv[:, t:t + 1]).then_inc(s_xh, 1)

            def high_parts(i, k, l):
                t0, nt = chunk(i)
                act.wait_ge(s_wx, NC * l + i + 1)
                if l or k:
                    act.wait_ge(s_st, 16 * ((NC - 1) * l + i))
                for j in range(nt):
                    act.activation(part_place(i, k, j, 0), P[0:TR, 6 + j // 2, (j % 2) * D:(j % 2 + 1) * D],
                                   ACT.Copy, scale=rdeg[:, bass.ds(t0 + j, 1)]).then_inc(s_ph, 1)

            act.wait_ge(s_rd, 1)
            chunks(act, lambda i, k: high_parts(i, k, 0))
            chunks(act, lambda i, k: high_parts(i, k, 1))

            def layer3(i, k):
                nt = chunk(i)[1]

                def copy_transposed(j):
                    o = first_of(i) + j
                    act.wait_ge(s_tr, o + 1)
                    act.activation(x1T[:, slot2(k, j), 0, :, :], P[:, 4 + slot2(k, j), 0:2 * TR]
                                   .rearrange("p (h n) -> p h n", h=2), ACT.Copy).then_inc(s_tc, 1)

                def copy_neighbour(j):
                    o = first_of(i) + j
                    act.wait_ge(s_bs, o + 1)
                    if k or j >= 2:
                        act.wait_ge(s_pl, 2 * NT + o - 1)
                    act.activation(neigh_row[slot2(k, j)], P[0:TR, 6 + slot2(k, j), D:2 * D], ACT.Copy,
                                   scale=1 / WS).then_inc(s_hn, 1)

                def high_part(j):
                    o = first_of(i) + j
                    act.wait_ge(s_sp, o + 1)
                    if k >= 3:
                        n = 8 * (o - slot2(k, j))
                        if k == 4 and j >= 2:
                            n = 24 * i + 8 * (1 + j - slot2(k, j))
                        act.wait_ge(s_st3[slot2(k, j)], n)
                    elif o >= 2:
                        act.wait_ge(s_st3[o % 2], 16 * (o // 2))
                    act.activation(last_part(i, k, j, 0), neigh_row[slot2(k, j)], ACT.Copy
                                   ).then_inc(s_ph, 1)

                for j in range(0, nt, 2):
                    if j == 0:
                        for jj in range(min(2, nt)):
                            copy_transposed(jj)
                    for jj in range(j, min(j + 2, nt)):
                        copy_neighbour(jj)
                    for jj in range(j + 2, min(j + 4, nt)):
                        copy_transposed(jj)
                    for jj in range(j, min(j + 2, nt)):
                        high_part(jj)

            chunks(act, layer3)

        @block.vector
        def _(dve):
            done = [0]

            def link(ins):
                done[0] += 1
                ins.then_inc(s_v, 1)
                dve.wait_ge(s_v, done[0])

            dve.memset(ints[:, 0, (GK - 1) * GE:], 0)
            dve.memset(ints[:, 1, (GK - 1) * GE:], NOWHERE)
            dve.memset(lastd, 0)
            dve.memset(mhalf, -0.5)
            dve.memset(one16[:, :], 1.0)
            dve.memset(zero32[:, :], 0.0)
            link(dve.memset(steptab[:, :, NS:NSP], 0.0))
            dve.sem_inc(s_dc, 1)

            dve.memset(AT[:, 2 * ZP:2 * (ZP + ZD)].bitcast(F32), 0.0).then_inc(s_zero, 1)

            dve.wait_ge(s_edges, 16 * 6)
            dve.wait_ge(s_prev, 16 * GK)
            dve.wait_ge(s_pc, 1)
            srcf, dstf = flts[:, 0, :], flts[:, 1, :]
            lo16, key16, wd16 = (q16[:, q, :, :].rearrange("p k e -> p (k e)") for q in (1, 0, 2))
            dve.tensor_copy(gprev, lastd)
            link(dve.tensor_copy(flts, ints))
            scaled = ((hi, srcf, TR), (wd, dstf, WIN), (gprev, gprev, WIN))
            for a, b, size in scaled:
                last = dve.tensor_scalar(a, b, (size - 1) / 2, 1.0 / size, ALU.subtract, ALU.mult)
            link(last)
            for op in (ALU.add, ALU.subtract):
                for a, b, size in scaled:
                    last = dve.tensor_scalar(a, a, ROUND, None, op)
                link(last)
            dve.scalar_tensor_tensor(lo16, hi, -float(TR), srcf, ALU.mult, ALU.add)
            dve.tensor_copy(wd16, wd)
            dve.tensor_tensor(gend, wd.rearrange("p (k e) -> p k e", e=GE)[:, :, GE - 1], gidx, ALU.add)
            dve.scalar_tensor_tensor(gprev, gprev, -1.0, gidx, ALU.add, ALU.add)
            dve.tensor_copy(gcol16, gidx.unsqueeze(2).broadcast_to([128, GK, 128]))
            link(dve.scalar_tensor_tensor(dstf, wd, -float(WIN), dstf, ALU.mult, ALU.add))
            link(dve.scalar_tensor_tensor(key16, hi, float(WIN), dstf, ALU.mult, ALU.add))
            for k in range(GK):
                dve.tensor_scalar(ended[:, k, :], iota_s, gend[:, k:k + 1], None, ALU.is_gt)
                last = dve.tensor_scalar(grouphot[:, k, :], iota_s, gprev[:, k:k + 1], None, ALU.is_gt)
            link(last)
            link(dve.tensor_tensor(grouphot, grouphot, ended, ALU.subtract))
            dve.tensor_scalar(minus16[:, :], ident[:, 0:TR], -1.0, None, ALU.mult)
            dve.tensor_copy(ident16[:, :], ident[:, 0:TR]).then_inc(s_diag, 1)
            dve.wait_ge(s_sel, 1)

            def halves(a):
                return a.rearrange("p (b s) -> p b s", b=2)

            dve.tensor_copy(halves(steptab[:, 1, 0:NS]), P[:, 2:4, 0:SH]).then_inc(s_places, 1)
            link(dve.scalar_tensor_tensor(halves(bstep), P[:, 6:8, 0:SH], -1.0, halves(iota_s), ALU.mult, ALU.add))
            dve.tensor_scalar(steps_off[0:1, :], bstep[0:1, :], float(WIN), float(WIN * (NW - 1)),
                              ALU.mult, ALU.min)
            link(dve.tensor_tensor(halves(tmpk), halves(bstep), P[:, 4:6, 0:SH], ALU.is_equal))
            link(dve.scalar_tensor_tensor(halves(steptab[:, 0, 0:NS]), P[:, 0:2, 0:SH], 1.0, halves(tmpk),
                                          ALU.add, ALU.mult))
            dve.sem_inc(s_tab, 1)

            def keyhots(s, slot):
                dve.tensor_scalar(keyhot[:, slot, :], iota_key, steptab[:, 0, bass.ds(s, 1)], None,
                                  ALU.is_equal).then_inc(s_key, 1)

            for s in range(AHEAD):
                keyhots(s, s)
            dve.wait_ge(s_loops, 1)
            dve.sem_inc(s_add, 1)
            with dve.Fori(0, NS // UNROLL) as turn:
                s = turn * UNROLL
                _, place0 = nc.values_load_multi_w_load_instructions(
                    steps_off[0:1, bass.ds(s, UNROLL)], engines=[mybir.EngineType.DVE],
                    min_val=0, max_val=WIN * (NW - 1),
                    skip_runtime_bounds_check_because="windows are numbered 0 to NW - 1")
                for u in range(UNROLL):
                    if u + AHEAD in DVE_LO:
                        dve.tensor_scalar(lohot[:, (u + AHEAD) % LORING, 0:TR], iota_lo[:, 0:TR],
                                          steptab[:, 1, bass.ds(s + u + AHEAD, 1)], None, ALU.is_equal
                                          ).then_inc(s_dlo, 1)
                    keyhots(s + u + AHEAD, (u + AHEAD) % RING)
                    if u % ATONCE == 0:
                        dve.wait_ge(s_cp, BANKS + s + u + ATONCE)
                    dve.wait_ge(s_add, s + u + 1)
                    place = ATt[:, :, bass.ds(place0[u], WIN)]
                    dve.tensor_tensor(place, place, counted[:, u % RING, :]
                                      .rearrange("p (t c) -> p t c", c=WIN), ALU.add).then_inc(s_add, 1)

            dve.wait_ge(s_xws[0], 16 * (NT - XP + (XP + 1) // 2))
            dve.wait_ge(s_xws[1], 16 * (XP // 2))
            dve.memset(cols, 0.0)
            dve.wait_ge(s_wts, 16 * 5)
            link(dve.tensor_copy(BR[:, :, :], B12[:, :, :]))
            link(dve.tensor_tensor(BR[64:128, :, :], B12[64:128, :, :], BR[64:128, :, :], ALU.subtract))
            link(dve.tensor_scalar(W2p[:, :, 0, :], W[:, :, D:2 * D], WS, None, ALU.mult))
            link(dve.scalar_tensor_tensor(W2p[:, :, 1, :], W[:, :, D:2 * D], WS, W2p[:, :, 0, :],
                                          ALU.mult, ALU.subtract))
            for k in range(HB):
                last = dve.tensor_scalar(W3p[k][:, 0, :], W3[:, k, :], WS, None, ALU.mult)
            link(last)
            for k in range(HB):
                last = dve.scalar_tensor_tensor(W3p[k][:, 1, :], W3[:, k, :], WS, W3p[k][:, 0, :],
                                                ALU.mult, ALU.subtract)
            link(last)
            dve.tensor_reduce(blocksel[:, :], ident.rearrange("p (q t) -> p t q", q=4)[:, 0:NT, :],
                              axis=mybir.AxisListType.X, op=ALU.add)
            dve.wait_ge(s_dcol, 1)
            link(dve.tensor_scalar(deg, P[0:TR, 4, 0:NT], 1.0, None, ALU.add))
            dve.sem_inc(s_degc, 1)
            link(dve.tensor_scalar(rdeg, deg, WS, None, ALU.mult))
            link(dve.reciprocal(rdeg, rdeg))
            link(dve.tensor_scalar(rneigh, deg, -1.0, 1.0, ALU.add, ALU.max))
            link(dve.reciprocal(rneigh, rneigh))
            dve.sem_inc(s_rd, 1)

            for t in range(NT):
                dve.wait_ge(s_pow, 1 if t < FIRST else 2)
                dve.wait_ge(s_xh, t + 1)
                dve.scalar_tensor_tensor(Xt[0:TR, t, 1, :], St[0:TR, t % 8, :], dinv[:, t:t + 1],
                                         Xt[0:TR, t, 0, :], ALU.mult, ALU.subtract).then_inc(s_x1, 1)

            link(dve.tensor_tensor(sdeg, deg, dinv, ALU.mult))
            link(dve.tensor_copy(sd16[:, 0, :], sdeg))
            link(dve.tensor_tensor(sd16[:, 1, :], sdeg, sd16[:, 0, :], ALU.subtract))
            colsq = cols.rearrange("p (a q t) -> p a q t", a=2, q=2)
            for a in range(2):
                last = dve.tensor_copy(colsq[:, a, :, 0:NT], sd16)
            link(last)
            dve.sem_inc(s_sdc, 1)
            dve.wait_ge(s_sdt, 1)
            link(dve.tensor_copy(sdT16[:, :], P[:, 4, 0:TR]))

            def diagonals(i):
                t0, nt = chunk(i)
                for j in range(nt):
                    last = dve.tensor_scalar(DGt[:, j, :], sdT16[:, :], blocksel[:, bass.ds(t0 + j, 1)],
                                             None, ALU.mult)
                last.then_inc(s_dg, 1)

            def low_parts(i, k, l):
                t0, nt = chunk(i)
                for j in range(nt):
                    if j % 2 == 0:
                        dve.wait_ge(s_ph, NT * l + first_of(i) + min(j + 2, nt))
                    dve.scalar_tensor_tensor(part_place(i, k, j, 1),
                                             P[0:TR, 6 + j // 2, (j % 2) * D:(j % 2 + 1) * D],
                                             rdeg[:, bass.ds(t0 + j, 1)], part_place(i, k, j, 0),
                                             ALU.mult, ALU.subtract).then_inc(s_pl, 1)

            def layer12(i, k, l):
                nt = chunk(i)[1]
                li = NC * l + i
                if k != 1:
                    if l or k:
                        dve.wait_ge(s_used, NC * li)
                    diagonals(i)
                dve.wait_ge(s_used, NC * (li + 1))
                if l or k:
                    dve.wait_ge(s_wx, li)
                b = 2 * ((NC * l + k) % 2)
                z = P[:, b:b + 2, 0:nt * TR]
                dve.tensor_scalar(hT[:, 0, :, 0:nt * TR], z, 0.0, None, ALU.max).then_inc(s_hhi, 1)
                dve.wait_ge(s_hhi, li + 1)
                dve.scalar_tensor_tensor(hT[:, 1, :, 0:nt * TR], z, 0.0, hT[:, 0, :, 0:nt * TR],
                                         ALU.max, ALU.subtract).then_inc(s_h, 1)
                if k == 0:
                    diagonals(1)
                low_parts(i, k, l)

            chunks(dve, lambda i, k: layer12(i, k, 0))

            dve.wait_ge(s_wn, 32)
            for k in range(HB):
                last = dve.tensor_scalar(W4p[k][0], W4raw[:, k, :], WS, None, ALU.mult)
            link(last)
            for k in range(HB):
                last = dve.scalar_tensor_tensor(W4p[k][1], W4raw[:, k, :], WS, W4p[k][0], ALU.mult, ALU.subtract)
            link(last)
            dve.sem_inc(s_w4, 1)

            chunks(dve, lambda i, k: layer12(i, k, 1))

            def normalise(i, k, before, bank, scale, ready, apart=False):
                t0, nt = chunk(i)
                base = done[0]

                def finish(h, a, b):
                    dve.wait_ge(s_rs, before + h + 1)
                    dve.wait_ge(s_mv, before + h + 1)
                    for j in range(a, b):
                        dve.tensor_scalar(ring_tile(k, j), ring_tile(k, j), mv[0:TR, j, 0:1], rstd[0:TR, j:j + 1],
                                          ALU.subtract, ALU.mult).then_inc(s_ln, 1)

                for h, (a, b) in enumerate(pairs(nt)):
                    ready(h)
                    for j in range(a, b):
                        last = dve.scalar_tensor_tensor(ring_tile(k, j),
                                                        P[0:TR, bank + j // 2, (j % 2) * D:(j % 2 + 1) * D],
                                                        scale[:, bass.ds(t0 + j, 1)], ring_tile(k, j),
                                                        ALU.mult, ALU.add)
                    last.then_inc(s_aev, 1)
                    dve.wait_ge(s_aev, before + h + 1)
                    for j in range(a, b):
                        last = dve.bn_stats(stats[0:TR, j, :], ring_tile(k, j))
                    last.then_inc(s_v, 1)
                    dve.wait_ge(s_v, base + before + h + 1)
                    dve.nop(nofuse=True)
                    for j in range(a, b):
                        last = dve.bn_aggr(mv[0:TR, j, :], stats[0:TR, j, :])
                    last.then_inc(s_mv, 1)
                    if apart:
                        finish(h, a, b)
                if not apart:
                    for h, (a, b) in enumerate(pairs(nt)):
                        finish(h, a, b)

            rounds = TOPK // 8

            def layer3(i, k):
                nt = chunk(i)[1]
                for c in (0, 1) if k == 0 else () if k == 1 else (i,):
                    kc = c if k < 2 else k
                    dve.wait_ge(s_used, NC * (2 * NC + c + 1))
                    dve.wait_ge(s_xb, c + 1)
                    normalise(c, kc, pairs_before(c), 2 * ((2 * NC + kc) % 2), dinv, lambda h: None)

                def base(j):
                    dve.wait_ge(s_hh, first_of(i) + j + 1)
                    dve.scalar_tensor_tensor(ring_tile(k, j), P[0:TR, 6 + slot2(k, j), 0:D], 1 / WS,
                                             ring_tile(k, j), ALU.mult, ALU.add).then_inc(s_bs, 1)

                def low_transposed(j):
                    o = first_of(i) + j
                    dve.wait_ge(s_tc, o + 1)
                    high, low = (x1T[:, slot2(k, j), a, :, :] for a in range(2))
                    dve.tensor_tensor(low, P[:, 4 + slot2(k, j), 0:2 * TR].rearrange("p (h n) -> p h n", h=2),
                                      high, ALU.subtract).then_inc(s_tl, 1)

                for j in range(min(2, nt)):
                    low_transposed(j)

                for j0 in range(0, nt, 2):
                    pair = range(j0, min(j0 + 2, nt))
                    for j in pair:
                        base(j)
                    for j in range(j0 + 2, min(j0 + 4, nt)):
                        low_transposed(j)
                    n = 2 * rounds * (first_of(i) + j0)
                    m = len(pair)
                    dve.wait_ge(s_hn, first_of(i) + pair[-1] + 1)
                    dve.nop(nofuse=True)
                    for r in range(rounds):
                        for j in pair:
                            v = j - j0
                            row = neigh_left[v] if r else neigh_row[slot2(k, j)]
                            if r:
                                dve.wait_ge(s_topk, n + 2 * m * r - m + v + 1)
                                dve.nop(nofuse=True)
                            dve.max(top8[0:TR, v, r, :], row).then_inc(s_topk, 1)
                        for j in pair:
                            v = j - j0
                            row = neigh_left[v] if r else neigh_row[slot2(k, j)]
                            dve.wait_ge(s_topk, n + 2 * m * r + v + 1)
                            dve.nop(nofuse=True)
                            dve.match_replace(neigh_left[v], top8[0:TR, v, r, :], row, GONE).then_inc(s_topk, 1)
                    for j in pair:
                        dve.wait_ge(s_topk, n + 2 * m * rounds - m + (j - j0) + 1)
                        dve.scalar_tensor_tensor(neigh_row[slot2(k, j)], neigh_left[j - j0], GONE,
                                                 neigh_row[slot2(k, j)], ALU.is_le, ALU.mult).then_inc(s_sp, 1)

            chunks(dve, layer3)

            def layer4(i, k):
                def ready(h):
                    if k < 2:
                        dve.wait_ge(s_used, 3 * NC * NC + 2 * NC - 1 + k)
                    else:
                        dve.wait_ge(s_used, 3 * NC * NC + 2 * NC * (i - 1) + NC * (h + 1))

                dve.wait_ge(s_xr[k % 2], 16 * (4 - k % 2) + 8 * (i + 2 - k % 2))
                normalise(i, k, PAIRS + pairs_before(i), 2 * ((3 * NC + k) % 2), rneigh, ready, k >= 2)

            chunks(dve, layer4)

        @block.tensor
        def _(pe):
            def transpose_x(t):
                n = 16 * (t // 3 + 1) if isinstance(t, int) else 16 * (t - XP + 1 + (XP + 2) // 3)
                pe.wait_ge(s_xin[xslot(t, 3)], n)
                if not isinstance(t, int) or t >= 2:
                    pe.wait_ge(s_xtc, xbefore(t, 2))
                for h in range(2):
                    last = pe.transpose(P[:, 4 + xslot(t, 2), h * TR:(h + 1) * TR],
                                        x_tile[:, xslot(t, 3), 128 * h:128 * h + 128], ident[0:TR, 0:TR])
                last.then_inc(s_xt, 1)

            def multiply_x(t, halves):
                if 0 in halves:
                    pe.wait_ge(s_xtc, t + 1)
                    if not isinstance(t, int) or t >= 2:
                        pe.wait_ge(s_xmc, xbefore(t, 2))
                for h in halves:
                    last = pe.matmul(P[0:TR, 6 + xslot(t, 2), 0:D], xT[:, xslot(t, 2), h, :], W[:, h, 0:D],
                                     start=h == 0, stop=h == 1)
                if 1 in halves:
                    last.then_inc(s_xm, 1)

            pe.wait_ge(s_ident, 1)
            transpose_x(0)
            pe.wait_ge(s_w1, 16)
            for t in range(XP):
                if t + 1 < XP:
                    transpose_x(t + 1)
                multiply_x(t, (0, 1))
            pe.wait_ge(s_xmc, XP)

            pe.wait_ge(s_diag, 1)
            for q in range(4):
                for b in range(2):
                    for k in range(GK):
                        n = GL if k == GK - 1 else 128
                        lhs = gcol16[0:n, k, :] if q == 3 else q16[0:n, q, k, :]
                        last = pe.matmul(P[:, 2 * q + b, 0:SH], lhs, grouphot[0:n, k, b * SH:(b + 1) * SH],
                                         start=k == 0, stop=k == GK - 1)
            last.then_inc(s_sel, 1)

            pe.wait_ge(s_tab, 1)
            pe.sem_inc(s_cnt, LORING)
            with pe.Fori(0, NS // UNROLL) as turn:
                s = turn * UNROLL
                for u in range(UNROLL):
                    pe.wait_ge(s_key, s + u + 1)
                    if u in DVE_LO:
                        pe.wait_ge(s_dlo, len(DVE_LO) * turn + DVE_LO.index(u) + 1)
                    else:
                        pe.wait_ge(s_lo, turn * PER_TURN + u + 2 - sum(v < u for v in DVE_LO))
                    pe.wait_ge(s_cp, s + u + 1)
                    pe.matmul(P[:, u % BANKS, 0:KEYS], lohot[:, u % LORING, :], keyhot[:, u % RING, :],
                              start=True, stop=True).then_inc(s_cnt, 1)
                    if u == UNROLL // 8:
                        transpose_x(turn + XP)
                    if u == UNROLL // 2:
                        multiply_x(turn + XP, (0,))
                    if u == UNROLL // 2 + 2:
                        multiply_x(turn + XP, (1,))

            pe.wait_ge(s_sums, 16 * 3)
            for t in range(NT):
                last = pe.matmul(P[0:TR, 4, t:t + 1], sums[:, t * TR:(t + 1) * TR], one16[0:3 * NT, 0:1],
                                 start=True, stop=True)
            last.then_inc(s_dcol, 1)

            def agg_group(k, l, t0, tiles, tile, n, first, final):
                nt = tiles[1]
                for u in range(n):
                    t = tile + u
                    if l < 2:
                        rhs = AT[0:TR, bass.ds(t * AC + t0 * TR, nt * TR)]
                        for h in range(2):
                            for a in range(2):
                                lhs = X[0:TR, bass.ds(t * 2 * D + a * D + h * 128, 128)]
                                last = pe.matmul(P[:, 2 * (k % 2) + h, 0:nt * TR], lhs, rhs,
                                                 start=first and u == 0 and a == 0,
                                                 stop=final and u == n - 1 and a == 1)
                    else:
                        for j in range(*tiles):
                            lhs = AT[0:TR, bass.ds(t * AC + (t0 + j) * TR, TR)]
                            for a in range(2):
                                rhs = X[0:TR, bass.ds(t * 2 * D + a * D, D)]
                                last = pe.matmul(P[0:TR, 2 * (k % 2) + j // 2, (j % 2) * D:(j % 2 + 1) * D],
                                                 lhs, rhs, start=first and u == 0 and a == 0 and j % 2 == 0,
                                                 stop=final and u == n - 1 and a == 1
                                                 and (j % 2 == 1 or j == nt - 1))
                return last

            def aggregate(i, k, l, between, groups=range(NC), tiles=None):
                t0, nt = chunk(i)
                tiles = tiles or (0, nt)
                kk = NC * l + k
                for q in groups:
                    if k == 0 and l == 0:
                        pe.wait_ge(s_x1, 4 * q + 1)
                    elif k == 0 and q == NC - 1:
                        pe.wait_ge(s_ph, NT * l)
                        pe.wait_ge(s_pl, NT * l)
                    elif k == 0:
                        pe.wait_ge(s_re[q], 16 * l)
                    if l == 3 and q == NC - 1:
                        for j in range(*tiles):
                            for a in range(2):
                                pe.matmul(P[0:TR, 2 * (kk % 2) + j // 2, (j % 2) * D:(j % 2 + 1) * D],
                                          minus16[0:TR, :], X[0:TR, bass.ds((t0 + j) * 2 * D + a * D, D)],
                                          start=False, stop=False)
                    last = agg_group(kk, l, t0, tiles, 0 if q == 0 else 4 * q - 3, 1 if q == 0 else CT,
                                     q == 0, q == NC - 1)
                    last.then_inc(s_used, 1)
                    between(q)

            def diag_bias(bank, l, nt):
                for h in range(2):
                    pe.matmul(P[:, bank + h, 0:nt * TR], BR[:, l, 128 * h:128 * h + 128], DG16[:, 0:nt * TR],
                              start=False, stop=False)

            def next_operand(i, l):
                nt = chunk(i)[1]
                pe.wait_ge(s_h, NC * l + i + 1)
                if not (isinstance(i, int) and i == 0 and l == 0):
                    pe.wait_ge(s_pl, NT * l + first_of(i))
                for j in range(nt):
                    for kt in range(2):
                        for a, b in PRODUCTS:
                            w = W2p[:, kt, b, :] if l == 0 else W3p[kt][:, b, :]
                            last = pe.matmul(P[0:TR, 6 + j // 2, (j % 2) * D:(j % 2 + 1) * D],
                                             hT[:, a, kt, j * TR:(j + 1) * TR], w,
                                             start=kt == 0 and (a, b) == PRODUCTS[0],
                                             stop=kt == 1 and (a, b) == PRODUCTS[-1])
                last.then_inc(s_wx, 1)

            def before(i, k):
                return (i - 1, k - 1) if k else (NC - 1, NC - 1)

            def layer12(i, k, l):
                def between(q):
                    if l == 0 and k == 0 and q == 4:
                        pe.wait_ge(s_sdc, 1)
                        pe.transpose(P[:, 4, 0:TR], cols, ident[0:TR, 0:TR]).then_inc(s_sdt, 1)
                    if (l or k) and q == 3:
                        next_operand(before(i, k)[0], l if k else 0)
                    if q == 5:
                        pe.wait_ge(s_dg, NC * l + i + 1)
                        diag_bias(2 * ((NC * l + k) % 2), l, chunk(i)[1])
                if l or k >= 2:
                    pe.wait_ge(s_h, NC * l + i - 1)
                aggregate(i, k, l, between)

            def transpose_x1(i, k, j):
                o = first_of(i) + j
                pe.wait_ge(s_ln, o + 1)
                if k or j >= 2:
                    pe.wait_ge(s_tl, o - 1)
                for h in range(2):
                    last = pe.transpose(P[:, 4 + slot2(k, j), h * TR:(h + 1) * TR],
                                        ring_tile(k, j)[:, 128 * h:128 * h + 128], ident[0:TR, 0:TR])
                last.then_inc(s_tr, 1)

            def self_and_neighbour(i, k, j):
                o = first_of(i) + j
                pe.wait_ge(s_tl, o + 1)
                if k or j >= 2:
                    pe.wait_ge(s_bs, o - 1)
                    pe.wait_ge(s_hn, o - 1)
                for h in range(2):
                    for a, b in PRODUCTS:
                        last = pe.matmul(P[0:TR, 6 + slot2(k, j), :], x1T[:, slot2(k, j), a, h, :], W4p[h][b],
                                         start=h == 0 and (a, b) == PRODUCTS[0],
                                         stop=h == 1 and (a, b) == PRODUCTS[-1])
                last.then_inc(s_hh, 1)

            def tile_work(i, k, q, at=2):
                nt = chunk(i)[1]
                if q == at:
                    for j in range(min(nt, 2)):
                        transpose_x1(i, k, j)
                if q == at + 1:
                    for j in range(min(nt, 2)):
                        self_and_neighbour(i, k, j)
                    for j in range(2, nt):
                        transpose_x1(i, k, j)
                if q == at + 2:
                    for j in range(2, nt):
                        self_and_neighbour(i, k, j)

            def layer3(i, k):
                def between(q):
                    if k == 0 and q == 3:
                        next_operand(NC - 1, 1)
                    if k == 2:
                        tile_work(0, 0, q, 0)
                        tile_work(1, 1, q, 4)
                    if k >= 3:
                        tile_work(i - 1, k - 1, q)
                    if k == 0 and q == 3:
                        pe.wait_ge(s_w4, 1)
                pe.wait_ge(*((s_h, 2 * NC - 1 + i) if k < 2 else (s_aev, pairs_before(i - 1))))
                aggregate(i, k, 2, between)

            def layer4(i, k):
                if k == 0:
                    pe.wait_ge(s_aev, pairs_before(NC - 1))
                    aggregate(0, 0, 3, lambda q: tile_work(NC - 1, 4, q, 1), range(NC - 1))
                    pe.wait_ge(s_aev, PAIRS)
                    aggregate(1, 1, 3, lambda q: None, range(NC - 1))
                    aggregate(0, 0, 3, lambda q: None, [NC - 1])
                    aggregate(1, 1, 3, lambda q: None, [NC - 1])
                elif k > 1:
                    for h, tiles in enumerate(pairs(CT)):
                        pe.wait_ge(s_aev, PAIRS + (h + 1 if k == 2 else pairs_before(i - 1)))
                        aggregate(i, k, 3, lambda q: None, tiles=tiles)

            chunks(pe, lambda i, k: layer12(i, k, 0))
            chunks(pe, lambda i, k: layer12(i, k, 1))
            chunks(pe, layer3)
            chunks(pe, layer4)


def kernel(x, src, dst, L0_gnn_W1, L0_gnn_b1, L0_gnn_W2, L0_gnn_b2, L0_gnn_W3, L0_gnn_b3, L1_gnn_W_self,
           L1_gnn_W_neigh):
    import concourse.bacc as bacc
    from concourse.bass_utils import run_bass_kernel_spmd as run

    nc = bacc.Bacc("TRN2", target_bir_lowering=False, num_devices=1)
    arrays, args = {}, []
    given = [("x", x), ("src", src), ("dst", dst), ("w1", L0_gnn_W1), ("b1", L0_gnn_b1), ("w2", L0_gnn_W2),
             ("b2", L0_gnn_b2), ("w3", L0_gnn_W3), ("b3", L0_gnn_b3), ("wself", L1_gnn_W_self),
             ("wneigh", L1_gnn_W_neigh)]
    for name, a in given:
        a = np.ascontiguousarray(a)
        arrays[f"in_{name}"] = a
        args.append(nc.dram_tensor(f"in_{name}", a.shape, mybir.dt.from_np(a.dtype), kind="ExternalInput").ap())
    args.append(nc.dram_tensor("out", (N, D), F32, kind="ExternalOutput").ap())
    gnn(nc, *args)
    r = run(nc, [arrays], core_ids=[0])
    return r.results[0]["out"]
```
